# Optimizing a Trainium2 kernel written in Bass

```python
import numpy as np
import jax
import jax.numpy as jnp

def _softmax(x, axis=-1):
    return jax.nn.softmax(x, axis=axis)

def _gelu(x):
    return jax.nn.gelu(x, approximate=True)

def _silu(x):
    return jax.nn.silu(x)

def _sigmoid(x):
    return jax.nn.sigmoid(x)

def _layernorm(x, axis=-1, eps=1e-05):
    m = jnp.mean(x, axis=axis, keepdims=True)
    v = jnp.var(x, axis=axis, keepdims=True)
    return (x - m) / jnp.sqrt(v + eps)

def _scatter_add(tgt, idx, src, axis=0):
    return tgt.at[idx].add(src)

def _segment_sum(src, seg, n):
    return jax.ops.segment_sum(src, seg, n)
kernel_name = 'mk_prb_d1_jaxref_r4_fb2ecf'

def setup_inputs(seed: int=0):
    np.random.seed(seed)
    _w = jnp.asarray

    def _L0_attn_setup():
        import jax, jax.numpy as jnp
        import numpy as np
        B, L, DM = (4, 128, 256)
        DS, DC, EXP = (16, 4, 2)
        DI = EXP * DM
        DTR = (DM + 15) // 16
        EPS = 1e-12
        SLOPE = 0.01

        def _ln(x, w, b):
            m = x.mean(-1, keepdims=True)
            v = ((x - m) ** 2).mean(-1, keepdims=True)
            return (x - m) * jax.lax.rsqrt(v + EPS) * w + b

        def _mamba(x, in_proj_w, conv_w, conv_b, x_proj_w, dt_proj_w, dt_proj_b, A_log, D, out_proj_w):
            xz = jnp.einsum('bld,ed->ble', x, in_proj_w)
            xs, z = jnp.split(xz, 2, axis=-1)
            kern = conv_w.T[:, None, :]
            xs = jax.lax.conv_general_dilated(xs, kern, window_strides=(1,), padding=[(DC - 1, 0)], dimension_numbers=('NWC', 'WIO', 'NWC'), feature_group_count=DI)
            xs = jax.nn.silu(xs + conv_b)
            x_dbl = jnp.einsum('bld,ed->ble', xs, x_proj_w)
            dt_r = x_dbl[..., :DTR]
            Bm = x_dbl[..., DTR:DTR + DS]
            Cm = x_dbl[..., DTR + DS:]
            dt = jax.nn.softplus(jnp.einsum('blr,dr->bld', dt_r, dt_proj_w) + dt_proj_b)
            A = -jnp.exp(A_log)
            dA = jnp.exp(dt[..., None] * A)
            dBx = dt[..., None] * Bm[:, :, None, :] * xs[..., None]

            def step(h, inp):
                dA_t, dBx_t, C_t = inp
                h = dA_t * h + dBx_t
                y = jnp.einsum('bdn,bn->bd', h, C_t)
                return (h, y)
            h0 = jnp.zeros((x.shape[0], DI, DS), dtype=x.dtype)
            _, ys = jax.lax.scan(step, h0, (dA.transpose(1, 0, 2, 3), dBx.transpose(1, 0, 2, 3), Cm.transpose(1, 0, 2)))
            y = ys.transpose(1, 0, 2) + D * xs
            y = y * jax.nn.silu(z)
            return jnp.einsum('bld,ed->ble', y, out_proj_w)
        key = jax.random.key(seed)
        ks = jax.random.split(key, 16)
        s = 0.02
        inp = {'x': jax.random.normal(ks[0], (B, L, DM), dtype=jnp.float32), 'in_proj_w': jax.random.normal(ks[1], (2 * DI, DM), dtype=jnp.float32) * s, 'conv_w': jax.random.normal(ks[2], (DI, DC), dtype=jnp.float32) * s, 'conv_b': jnp.zeros((DI,), dtype=jnp.float32), 'x_proj_w': jax.random.normal(ks[3], (DTR + 2 * DS, DI), dtype=jnp.float32) * s, 'dt_proj_w': jax.random.normal(ks[4], (DI, DTR), dtype=jnp.float32) * s, 'dt_proj_b': jax.random.normal(ks[5], (DI,), dtype=jnp.float32) * s, 'A_log': jnp.log(jnp.tile(jnp.arange(1, DS + 1, dtype=jnp.float32), (DI, 1))), 'D': jnp.ones((DI,), dtype=jnp.float32), 'out_proj_w': jax.random.normal(ks[6], (DM, DI), dtype=jnp.float32) * s, 'ln1_w': jnp.ones((DM,), dtype=jnp.float32), 'ln1_b': jnp.zeros((DM,), dtype=jnp.float32), 'ffn_w1': jax.random.normal(ks[7], (2 * DM, DM), dtype=jnp.float32) * s, 'ffn_b1': jnp.zeros((2 * DM,), dtype=jnp.float32), 'ffn_w2': jax.random.normal(ks[8], (DM, 2 * DM), dtype=jnp.float32) * s, 'ffn_b2': jnp.zeros((DM,), dtype=jnp.float32), 'ln2_w': jnp.ones((DM,), dtype=jnp.float32), 'ln2_b': jnp.zeros((DM,), dtype=jnp.float32)}
        return inp
    _L0_attn_in = _L0_attn_setup()

    def _L0_ffn_setup():
        import jax, jax.numpy as jnp
        import numpy as np
        D_MODEL = 256
        D_FF = 1024
        N_EXPERTS = 8
        D_EXPERT = D_FF // N_EXPERTS
        TOP_K = 2
        LB_WEIGHT = 0.01
        B, S = (4, 512)

        def _top_k_softmax(logits, k):
            vals, _ = jax.lax.top_k(logits, k)
            thresh = vals[..., -1:]
            masked = jnp.where(logits >= thresh, logits, -jnp.inf)
            return jax.nn.softmax(masked, axis=-1)
        key = jax.random.key(seed)
        ks = jax.random.split(key, 8)
        x = jax.random.normal(ks[0], (B, S, D_MODEL), dtype=jnp.float32)
        w1 = jax.random.normal(ks[1], (N_EXPERTS, D_MODEL, D_EXPERT), dtype=jnp.float32) * (1.0 / np.sqrt(D_MODEL))
        b1 = jnp.zeros((N_EXPERTS, D_EXPERT), dtype=jnp.float32)
        w2 = jax.random.normal(ks[2], (N_EXPERTS, D_EXPERT, D_MODEL), dtype=jnp.float32) * (1.0 / np.sqrt(D_EXPERT))
        b2 = jnp.zeros((N_EXPERTS, D_MODEL), dtype=jnp.float32)
        centroids = jax.random.normal(ks[3], (N_EXPERTS, D_MODEL), dtype=jnp.float32) * 0.02
        w_route = jax.random.normal(ks[4], (N_EXPERTS, D_MODEL), dtype=jnp.float32) * (1.0 / np.sqrt(D_MODEL))
        return {'x': x, 'w1': w1, 'b1': b1, 'w2': w2, 'b2': b2, 'centroids': centroids, 'w_route': w_route}
    _L0_ffn_in = _L0_ffn_setup()
    _d = {'L0_attn_x': _L0_attn_in['x'], 'L0_attn_in_proj_w': _L0_attn_in['in_proj_w'], 'L0_attn_conv_w': _L0_attn_in['conv_w'], 'L0_attn_conv_b': _L0_attn_in['conv_b'], 'L0_attn_x_proj_w': _L0_attn_in['x_proj_w'], 'L0_attn_dt_proj_w': _L0_attn_in['dt_proj_w'], 'L0_attn_dt_proj_b': _L0_attn_in['dt_proj_b'], 'L0_attn_A_log': _L0_attn_in['A_log'], 'L0_attn_D': _L0_attn_in['D'], 'L0_attn_out_proj_w': _L0_attn_in['out_proj_w'], 'L0_attn_ln1_w': _L0_attn_in['ln1_w'], 'L0_attn_ln1_b': _L0_attn_in['ln1_b'], 'L0_attn_ffn_w1': _L0_attn_in['ffn_w1'], 'L0_attn_ffn_b1': _L0_attn_in['ffn_b1'], 'L0_attn_ffn_w2': _L0_attn_in['ffn_w2'], 'L0_attn_ffn_b2': _L0_attn_in['ffn_b2'], 'L0_attn_ln2_w': _L0_attn_in['ln2_w'], 'L0_attn_ln2_b': _L0_attn_in['ln2_b'], 'L0_ffn_w1': _L0_ffn_in['w1'], 'L0_ffn_b1': _L0_ffn_in['b1'], 'L0_ffn_w2': _L0_ffn_in['w2'], 'L0_ffn_b2': _L0_ffn_in['b2'], 'L0_ffn_centroids': _L0_ffn_in['centroids'], 'L0_ffn_w_route': _L0_ffn_in['w_route']}
    _x0 = _d['L0_attn_x']
    _d['L0_attn_x'] = jax.random.normal(jax.random.fold_in(jax.random.key(seed), 1), (8, 1024, 256), dtype=_x0.dtype)
    del _x0
    return _d

def reference(L0_attn_x, L0_attn_in_proj_w, L0_attn_conv_w, L0_attn_conv_b, L0_attn_x_proj_w, L0_attn_dt_proj_w, L0_attn_dt_proj_b, L0_attn_A_log, L0_attn_D, L0_attn_out_proj_w, L0_attn_ln1_w, L0_attn_ln1_b, L0_attn_ffn_w1, L0_attn_ffn_b1, L0_attn_ffn_w2, L0_attn_ffn_b2, L0_attn_ln2_w, L0_attn_ln2_b, L0_ffn_w1, L0_ffn_b1, L0_ffn_w2, L0_ffn_b2, L0_ffn_centroids, L0_ffn_w_route):

    def _L0_attn_ref(x, in_proj_w, conv_w, conv_b, x_proj_w, dt_proj_w, dt_proj_b, A_log, D, out_proj_w, ln1_w, ln1_b, ffn_w1, ffn_b1, ffn_w2, ffn_b2, ln2_w, ln2_b):
        import jax, jax.numpy as jnp
        import numpy as np
        B, L, DM = (4, 128, 256)
        DS, DC, EXP = (16, 4, 2)
        DI = EXP * DM
        DTR = (DM + 15) // 16
        EPS = 1e-12
        SLOPE = 0.01

        def _ln(x, w, b):
            m = x.mean(-1, keepdims=True)
            v = ((x - m) ** 2).mean(-1, keepdims=True)
            return (x - m) * jax.lax.rsqrt(v + EPS) * w + b

        def _mamba(x, in_proj_w, conv_w, conv_b, x_proj_w, dt_proj_w, dt_proj_b, A_log, D, out_proj_w):
            xz = jnp.einsum('bld,ed->ble', x, in_proj_w)
            xs, z = jnp.split(xz, 2, axis=-1)
            kern = conv_w.T[:, None, :]
            xs = jax.lax.conv_general_dilated(xs, kern, window_strides=(1,), padding=[(DC - 1, 0)], dimension_numbers=('NWC', 'WIO', 'NWC'), feature_group_count=DI)
            xs = jax.nn.silu(xs + conv_b)
            x_dbl = jnp.einsum('bld,ed->ble', xs, x_proj_w)
            dt_r = x_dbl[..., :DTR]
            Bm = x_dbl[..., DTR:DTR + DS]
            Cm = x_dbl[..., DTR + DS:]
            dt = jax.nn.softplus(jnp.einsum('blr,dr->bld', dt_r, dt_proj_w) + dt_proj_b)
            A = -jnp.exp(A_log)
            dA = jnp.exp(dt[..., None] * A)
            dBx = dt[..., None] * Bm[:, :, None, :] * xs[..., None]

            def step(h, inp):
                dA_t, dBx_t, C_t = inp
                h = dA_t * h + dBx_t
                y = jnp.einsum('bdn,bn->bd', h, C_t)
                return (h, y)
            h0 = jnp.zeros((x.shape[0], DI, DS), dtype=x.dtype)
            _, ys = jax.lax.scan(step, h0, (dA.transpose(1, 0, 2, 3), dBx.transpose(1, 0, 2, 3), Cm.transpose(1, 0, 2)))
            y = ys.transpose(1, 0, 2) + D * xs
            y = y * jax.nn.silu(z)
            return jnp.einsum('bld,ed->ble', y, out_proj_w)
        h = _mamba(x, in_proj_w, conv_w, conv_b, x_proj_w, dt_proj_w, dt_proj_b, A_log, D, out_proj_w)
        h = _ln(h + x, ln1_w, ln1_b)
        f = jnp.einsum('bld,ed->ble', h, ffn_w1) + ffn_b1
        f = jnp.where(f >= 0, f, SLOPE * f)
        f = jnp.einsum('ble,de->bld', f, ffn_w2) + ffn_b2
        return _ln(f + h, ln2_w, ln2_b)

    def _L0_ffn_ref(x, w1, b1, w2, b2, centroids, w_route):
        import jax, jax.numpy as jnp
        import numpy as np
        D_MODEL = 256
        D_FF = 1024
        N_EXPERTS = 8
        D_EXPERT = D_FF // N_EXPERTS
        TOP_K = 2
        LB_WEIGHT = 0.01
        B, S = (4, 512)

        def _top_k_softmax(logits, k):
            vals, _ = jax.lax.top_k(logits, k)
            thresh = vals[..., -1:]
            masked = jnp.where(logits >= thresh, logits, -jnp.inf)
            return jax.nn.softmax(masked, axis=-1)
        eps = 1e-12
        x_norm = x / jnp.maximum(jnp.linalg.norm(x, axis=-1, keepdims=True), eps)
        c_norm = centroids / jnp.maximum(jnp.linalg.norm(centroids, axis=-1, keepdims=True), eps)
        cos_scores = jnp.einsum('bsd,ed->bse', x_norm, c_norm)
        route_scores = jnp.einsum('bsd,ed->bse', x, w_route)
        logits = cos_scores + route_scores
        gates = _top_k_softmax(logits, TOP_K)
        h = jax.nn.gelu(jnp.einsum('bsd,edh->bseh', x, w1) + b1, approximate=False)
        expert_out = jnp.einsum('bseh,ehd->bsed', h, w2) + b2
        out = jnp.einsum('bse,bsed->bsd', gates, expert_out)
        return out
    x = L0_attn_x
    xn = _layernorm(x, axis=-1)
    x = x + _L0_attn_ref(xn, L0_attn_in_proj_w, L0_attn_conv_w, L0_attn_conv_b, L0_attn_x_proj_w, L0_attn_dt_proj_w, L0_attn_dt_proj_b, L0_attn_A_log, L0_attn_D, L0_attn_out_proj_w, L0_attn_ln1_w, L0_attn_ln1_b, L0_attn_ffn_w1, L0_attn_ffn_b1, L0_attn_ffn_w2, L0_attn_ffn_b2, L0_attn_ln2_w, L0_attn_ln2_b) + _L0_ffn_ref(xn, L0_ffn_w1, L0_ffn_b1, L0_ffn_w2, L0_ffn_b2, L0_ffn_centroids, L0_ffn_w_route)
    return x

_drawn_inputs = setup_inputs


def setup_inputs(seed=0):
    import zlib

    import numpy as np

    out = dict(_drawn_inputs(seed))
    spreads = {'L0_attn_conv_b': (0.0, 0.8),
     'L0_attn_D': (1.0, 0.6),
     'L0_attn_ln1_w': (1.0, 0.2),
     'L0_attn_ln1_b': (0.0, 0.1),
     'L0_attn_ffn_b1': (0.0, 0.554),
     'L0_attn_ffn_b2': (0.0, 0.1),
     'L0_attn_ln2_w': (1.0, 0.2),
     'L0_attn_ln2_b': (0.0, 0.1),
     'L0_ffn_b1': (0.0, 0.334),
     'L0_ffn_b2': (0.0, 0.1)}
    factors = {'L0_attn_in_proj_w': 8.0,
     'L0_attn_conv_w': 8.0,
     'L0_attn_x_proj_w': 8.0,
     'L0_attn_dt_proj_w': 8.0,
     'L0_attn_dt_proj_b': 8.0,
     'L0_attn_A_log': 8.0,
     'L0_attn_out_proj_w': 8.0}
    for name, (base, spread) in spreads.items():
        noise = np.random.default_rng([zlib.crc32(name.encode()), seed]).standard_normal(out[name].shape)
        drawn = base * np.exp(spread * noise) if base else spread * noise
        out[name] = jnp.asarray(drawn.astype(out[name].dtype))
    for name, factor in factors.items():
        out[name] = (out[name] * factor).astype(out[name].dtype)
    return out
```

```python
from contextlib import ExitStack

import numpy as np

import concourse.bass as bass
from concourse import mybir

F32 = mybir.dt.float32
BF16 = mybir.dt.bfloat16
ALU = mybir.AluOpType
ACT = mybir.ActivationFunctionType
AX = mybir.AxisListType

P = 128


class Stage:

    def __init__(self, sem, step=1):
        self.sem, self.step, self.count = sem, step, 0


class Ring:

    def __init__(self, bufs):
        self.bufs, self.free, self.turn = bufs, [None] * len(bufs), -1

    def take(self):
        self.turn += 1
        i = self.turn % len(self.bufs)
        return i, self.bufs[i], self.free[i]


def build_block(nc: bass.Bass, x, win, wconv, bconv, wx, wdt, alog, dvec, wout, ln1, f1, fb1, f2, fb2,
                ln2, m1, mb1, m2, mb2, cent, wroute, ident_in, identb_in, sel_in, out):
    B, L, DM = x.shape
    K = DM // P
    DI = win.shape[2] // 2
    G = DI // P
    DC = wconv.shape[2]
    DTR = wdt.shape[0] - 1
    DS = alog.shape[2]
    XW = DTR + 2 * DS
    F = f1.shape[2] // P
    E = m1.shape[2]
    SW = 3 * DS
    T = 512
    J = T // P
    NC = B * L // T
    CPS = L // T
    STEPS = DS * G

    x_c = x.rearrange("b (h j p) d -> (b h) p j d", j=J, p=P)
    out_c = out.rearrange("b (h j p) d -> (b h) p j d", j=J, p=P)

    ctx = ExitStack()
    with ctx:
        def sb(name, shape, dt=F32):
            return ctx.enter_context(nc.sbuf_tensor(name, shape, dt))

        def stage(name, step=1):
            return Stage(ctx.enter_context(nc.semaphore("s_" + name)), step)

        win_s = sb("win_s", [P, K, 2 * DI])
        wconv_s = sb("wconv_s", [P, G, DC])
        bconv_s = sb("bconv_s", [P, G])
        wx_s = sb("wx_s", [P, G, XW])
        wdt_s = sb("wdt_s", [DTR + 1, DI])
        alog_s = sb("alog_s", [P, G, DS])
        nega = sb("nega", [P, G, DS])
        d_s = sb("d_s", [P, G])
        wout_s = sb("wout_s", [P, G, DM])
        ln1_s = sb("ln1_s", [P, 2, DM])
        ln2_s = sb("ln2_s", [P, 2, DM])
        f1_s = sb("f1_s", [P, K, F * P])
        fb1_s = sb("fb1_s", [P, F])
        f2_s = sb("f2_s", [P, F, DM])
        fb2_s = sb("fb2_s", [1, DM])
        m1_s = sb("m1_s", [P, K, E, P])
        mb1_s = sb("mb1_s", [P, E])
        m2_s = sb("m2_s", [P, E, DM])
        mb2_s = sb("mb2_s", [E, DM])
        wrc_s = sb("wrc_s", [P, K, 2 * E])
        ident = sb("ident", [P, P])
        identb = sb("identb", [P, P], BF16)
        sel = sb("sel", [SW, DS, P], BF16)
        ones = sb("ones", [1, P])
        mhalf = sb("mhalf", [P, J])
        dconv = sb("dconv", [P, G, DC, P])
        dskip = sb("dskip", [P, G, P])
        css = sb("css", [E, 2])

        xn = [sb(f"xn{i}", [P, J, DM]) for i in range(3)]
        xnT = [sb(f"xnT{i}", [P, K, T]) for i in range(3)]
        xpad = sb("xpad", [P, G, T + DC - 1])
        xs = [sb(f"xs{i}", [P, G, T]) for i in range(2)]
        dt = [sb(f"dt{i}", [P, G, T]) for i in range(2)]
        y = [sb(f"y{i}", [P, J, DI]) for i in range(2)]
        xdbl = [sb(f"xdbl{i}", [P, J, XW]) for i in range(2)]
        bT = [sb(f"bT{i}", [SW, T], BF16) for i in range(2)]
        bsp = sb("bsp", [P, J, SW], BF16)
        brem = sb("brem", [P, J, DS])
        dtrT = sb("dtrT", [DTR + 1, T])
        yT = sb("yT", [P, G, T])
        fT = yT
        h1 = sb("hres", [P, J, DM])
        cent_s = h1[0:E, 0, :]
        h1T = sb("hresT", [P, K, T])
        xres = h1T.ap().rearrange("p k t -> p (k t)").rearrange("p (j d) -> p j d", j=J) \
            if hasattr(h1T, "ap") else h1T[:, :, :].rearrange("p k t -> p (k t)").rearrange("p (j d) -> p j d", j=J)
        junk = sb("junk", [P, DM], BF16)
        gss = sb("gss", [P, J])
        ginv = sb("ginv", [P, J])
        glog = sb("glog", [P, J, 2 * E])
        gl = sb("gl", [P, J, E])
        gtop = sb("gtop", [P, J, 8])
        gmask = sb("gmask", [P, J, E])
        gex = sb("gex", [P, J, E])
        gsum = sb("gsum", [P, J])
        gate = [sb(f"gate{i}", [P, J, E]) for i in range(3)]
        grem = sb("grem", [P, J, E])
        gsp = sb("gsp", [P, J, SW], BF16)
        gT = sb("gT", [SW, T], BF16)
        gTf = sb("gTf", [E, T])
        small = {k: (sb(f"{k}_st", [P, J, 6]), sb(f"{k}_mv", [P, J, 2]), sb(f"{k}_ve", [P, J]), sb(f"{k}_rs", [P, J]))
                 for k in ("pre", "post")}
        carry = sb("carry", [P, DS, G])

        NDA, NH, NBU = 4, 4, 3
        dA = Ring([sb(f"dA{i}", [P, T]) for i in range(NDA)])
        h = Ring([sb(f"hs{i}", [P, T]) for i in range(NH)])
        bu = Ring([sb(f"bu{i}", [P, 2, T]) for i in range(NBU)])
        bbc = Ring([sb(f"bbc{i}", [P, T]) for i in range(2)])
        gbuf = Ring([sb(f"gbuf{i}", [P, T]) for i in range(2)])

        hT = [ctx.enter_context(nc.psum_tensor(f"hT{j}", [P, DI], F32)) for j in range(J)]
        acc = ctx.enter_context(nc.psum_tensor("acc", [P, J, DM], F32))
        bank = Ring([ctx.enter_context(nc.psum_tensor(f"bank{i}", [P, T], F32)) for i in range(2)])

        queue = {k: [] for k in ("sync", "pe", "dve", "act", "pool")}
        waited = {k: {} for k in queue}

        def emit(eng, make, done=None, after=()):
            for mark in after:
                if mark is None:
                    continue
                st, n = mark
                if waited[eng].get(st, 0) < n:
                    waited[eng][st] = n
                    queue[eng].append(lambda e, s=st.sem, n=n: e.wait_ge(s, n))
            if done is None:
                queue[eng].append(make)
                return None
            done.count += done.step
            queue[eng].append(lambda e, s=done: make(e).then_inc(s.sem, s.step))
            return done, done.count

        s_wfirst, s_wrest = stage("wfirst", 16), stage("wrest", 16)
        s_x = [stage(f"x{i}", 16) for i in range(3)]
        s_xres, s_out = stage("xres", 16), stage("out", 16)

        def load_x(c, after=()):
            return emit("sync", lambda e: e.dma_start(xn[c % 3][:, :, :], x_c[c]), s_x[c % 3], after)

        x_here = {0: load_x(0)}
        for dst, src in ((ident[:, :], ident_in), (win_s[:, :, :], win), (wconv_s[:, :, :], wconv),
                         (bconv_s[:, :], bconv), (d_s[:, :], dvec), (alog_s[:, :, :], alog),
                         (wx_s[:, :, :], wx), (wdt_s[:, :], wdt), (cent_s, cent),
                         (wrc_s[:, :, 0:E], wroute), (identb[:, :], identb_in), (sel[:, :, :], sel_in)):
            w_first = emit("sync", lambda e, d=dst, s=src: e.dma_start(d, s), s_wfirst)
        x_here[1] = load_x(1)
        for dst, src in ((m1_s[:, :, :, :], m1), (mb1_s[:, :], mb1), (m2_s[:, :, :], m2), (mb2_s[:, :], mb2),
                         (wout_s[:, :, :], wout), (ln1_s[:, :, :], ln1), (f1_s[:, :, :], f1), (fb1_s[:, :], fb1),
                         (f2_s[:, :, :], f2), (fb2_s[:, :], fb2), (ln2_s[:, :, :], ln2)):
            w_rest = emit("sync", lambda e, d=dst, s=src: e.dma_start(d, s), s_wrest)

        s_ms, s_cst, s_neg, s_css = stage("ms"), stage("cst"), stage("neg"), stage("css")
        emit("pool", lambda e: e.memset(mhalf[:, :], -0.5), s_ms)
        emit("pool", lambda e: e.memset(dtrT[:, :], 1.0), s_ms)
        emit("pool", lambda e: e.memset(gsp[:, :, :], 0.0), s_ms)
        memsets = emit("pool", lambda e: e.memset(ones[:, :], 1.0), s_ms)

        t = emit("act", lambda e: e.activation(nega[:, :, :], alog_s[:, :, :], ACT.Exp), s_neg, [w_first])
        css_sq = emit("act", lambda e: e.activation(junk[0:E, :], cent_s, ACT.Square, accum_out=css[:, 0:1]),
                      s_css, [w_first])
        cst_neg = emit("dve", lambda e: e.tensor_scalar(nega[:, :, :], nega[:, :, :], -1.0, None, ALU.mult),
                       s_cst, [t])
        for buf in (wconv_s[:, :, :], bconv_s[:, :], win_s[:, :, DI:2 * DI]):
            cst_half = emit("dve", lambda e, b=buf: e.tensor_scalar(b, b, 0.5, None, ALU.mult), s_cst, [w_first])
        for g in range(G):
            for k in range(DC):
                emit("dve", lambda e, g=g, k=k: e.tensor_scalar(dconv[:, g, k, :], ident[:, :], wconv_s[:, g, k:k + 1],
                                                                None, ALU.mult), s_cst, [cst_half])
            cst_diag = emit("dve", lambda e, g=g: e.tensor_scalar(dskip[:, g, :], ident[:, :], d_s[:, g:g + 1],
                                                                  None, ALU.mult), s_cst)
        t = emit("pool", lambda e: e.tensor_scalar(css[:, 1:2], css[:, 0:1], 1e-24, 1.0, ALU.max, ALU.mult),
                 s_css, [css_sq])
        t = emit("pool", lambda e: e.tensor_tensor(css[:, 0:1], css[:, 1:2], mhalf[0:E, 0:1], ALU.pow),
                 s_css, [t, memsets])
        t = emit("dve", lambda e: e.tensor_scalar(cent_s, cent_s, css[:, 0:1], None, ALU.mult),
                 s_cst, [t])
        i, ps, free = bank.take()
        for k in range(K):
            t2 = emit("pe", lambda e, k=k, ps=ps: e.transpose(ps[:, k * E:(k + 1) * E], cent_s[:, k * P:(k + 1) * P],
                                                              ident[0:E, 0:E]), s_css, [t, w_first])
        cst_cent = emit("dve", lambda e, ps=ps: e.tensor_copy(
            wrc_s[:, :, E:2 * E], ps[:, 0:K * E].rearrange("p (k e) -> p k e", k=K)), s_cst, [t2])
        bank.free[i] = cst_cent

        S = {n: stage(n) for n in (
            "ln_pre", "ln_post", "rs_pre", "rs_post", "tr", "ev", "inproj", "pad", "xpad", "conv", "silu", "silm",
            "xproj", "xdbl", "bsp", "btr", "bev", "dtmm", "dta", "dtb", "dtc", "u", "skip", "yinit",
            "gq", "rt", "gate", "gx", "gtr", "gev",
            "bbcmm", "bbc", "bu", "dA", "scan", "carry", "hT", "sum",
            "zmm", "sz", "szm", "yz", "ytr", "yev", "omm", "hres", "aff", "h1T", "f1mm", "f1a", "f1l", "f2mm",
            "m1mm", "gelu", "gbc", "mg", "m2mm", "fin")}
        last = {}

        def normalize(tag, buf, eps, ready):
            st, mv, ve, rs = small[tag]
            lnS, rsS = S["ln_" + tag], S["rs_" + tag]
            for j in range(J):
                t = emit("dve", lambda e, j=j: e.bn_stats(st[:, j, :], buf[:, j, :]), lnS, ready + [last.get(tag)])
            for j in range(J):
                t = emit("dve", lambda e, j=j: e.bn_aggr(mv[:, j, :], st[:, j, :]), lnS, [t])
            yield 0.1
            t = emit("pool", lambda e: e.tensor_scalar(ve[:, :], mv[:, :, 1], eps, 1.0, ALU.add, ALU.mult), rsS, [t])
            t = emit("pool", lambda e: e.tensor_tensor(rs[:, :], ve[:, :], mhalf[:, :], ALU.pow), rsS, [t, memsets])
            yield 0.1
            for j in range(J):
                t2 = emit("dve", lambda e, j=j: e.tensor_scalar(buf[:, j, :], buf[:, j, :], mv[:, j, 0:1], rs[:, j:j + 1],
                                                                ALU.subtract, ALU.mult), lnS, [t])
            last[tag] = t2

        def transposed(src, dst, ready, free_dst, pe_done, ev_done):
            for k in range(K):
                i, ps, free = bank.take()
                for j in range(J):
                    t = emit("pe", lambda e, k=k, j=j, ps=ps: e.transpose(
                        ps[:, j * P:(j + 1) * P], src[:, j, k * P:(k + 1) * P], ident[:, :]), pe_done, ready + [free, w_first])
                bank.free[i] = emit("act", lambda e, k=k, ps=ps: e.activation(dst[:, k, :], ps[:, :], ACT.Copy),
                                    ev_done, [t] + free_dst)
                yield 0.45
            last["tr"] = bank.free[i]

        def pre(c):
            b, p = c % 3, c % 2
            yield from normalize("pre", xn[b], 1e-5, [x_here[c]])
            xn_here = last["pre"]
            xn_ready[c] = xn_here
            yield from transposed(xn[b], xnT[b], [xn_here], [last.get(("xnT", b))], S["tr"], S["ev"])
            xnT_here = last["tr"]
            xnT_ready[c] = xnT_here
            for j in range(J):
                tq = emit("act", lambda e, j=j: e.activation(junk[:, :], xn[b][:, j, :], ACT.Square,
                                                             accum_out=gss[:, j:j + 1]), S["gq"],
                          [xn_here, last.get("gss"), last.get("junk")])
                last["junk"] = tq
            i, ps, free = bank.take()
            for j in range(J):
                for k in range(K):
                    t = emit("pe", lambda e, k=k, j=j, ps=ps: e.matmul(
                        ps[:, j * 2 * E:(j + 1) * 2 * E], xnT[b][:, k, j * P:(j + 1) * P], wrc_s[:, k, :],
                        start=(k == 0), stop=(k == K - 1)), S["gtr"], [xnT_here, free, cst_cent])
            bank.free[i] = tl = emit("dve", lambda e, ps=ps: e.tensor_copy(
                glog[:, :, :], ps[:, 0:J * 2 * E].rearrange("p (j e) -> p j e", j=J)), S["rt"], [t, last.get("glog")])
            last["xn_sq"] = tq
            yield 1.7
            tp = last.get("conv_read")
            if c % CPS:
                pad = emit("pool", lambda e: e.tensor_copy(xpad[:, :, 0:DC - 1], xpad[:, :, T:T + DC - 1]), S["pad"],
                           [tp, last.get("xpad_w")])
            else:
                pad = emit("pool", lambda e: e.memset(xpad[:, :, 0:DC - 1], 0.0), S["pad"], [tp])
            for g in range(G):
                i, ps, free = bank.take()
                for k in range(K):
                    t = emit("pe", lambda e, g=g, k=k, ps=ps: e.matmul(
                        ps[:, :], win_s[:, k, g * P:(g + 1) * P], xnT[b][:, k, :],
                        start=(k == 0), stop=(k == K - 1)), S["inproj"], [xnT_here, free])
                bank.free[i] = xw = emit("act", lambda e, g=g, ps=ps: e.activation(
                    xpad[:, g, DC - 1:], ps[:, :], ACT.Copy), S["xpad"], [t, tp, pad, last.get("relu_read")])
                yield 1.7
            last["xpad_w"] = xw
            for g in range(G):
                i, ps, free = bank.take()
                for k in range(DC):
                    t = emit("pe", lambda e, g=g, k=k, ps=ps: e.matmul(
                        ps[:, :], dconv[:, g, k, :], xpad[:, g, k:k + T], start=(k == 0), stop=(k == DC - 1)),
                        S["conv"], [xw, pad, free, cst_diag])
                last["conv_read"] = t
                gi, gb, gfree = gbuf.take()
                ta = emit("act", lambda e, g=g, ps=ps, gb=gb: e.activation(
                    gb[:, :], ps[:, :], ACT.Tanh, bias=bconv_s[:, g:g + 1]), S["silu"], [t, gfree, cst_half])
                bank.free[i] = ta = emit("act", lambda e, g=g, ps=ps: e.activation(
                    xs[p][:, g, :], ps[:, :], ACT.Identity, bias=bconv_s[:, g:g + 1]), S["silu"],
                    [last.get(("u_read", p))])
                gbuf.free[gi] = xs_here = emit("dve", lambda e, g=g, gb=gb: e.scalar_tensor_tensor(
                    out=xs[p][:, g, :], in0=gb[:, :], scalar=1.0, in1=xs[p][:, g, :], op0=ALU.add, op1=ALU.mult),
                    S["silm"], [ta])
                yield 3.4
            i, ps, free = bank.take()
            for j in range(J):
                for g in range(G):
                    t = emit("pe", lambda e, g=g, j=j, ps=ps: e.matmul(
                        ps[:, j * XW:(j + 1) * XW], xs[p][:, g, j * P:(j + 1) * P], wx_s[:, g, :],
                        start=(g == 0), stop=(g == G - 1)), S["xproj"], [xs_here, free])
            bank.free[i] = xd = emit("dve", lambda e, ps=ps: e.tensor_copy(
                xdbl[p][:, :, :], ps[:, 0:J * XW].rearrange("p (j e) -> p j e", j=J)), S["xdbl"],
                [t, last.get(("C_read", p))])
            yield 3.4
            i, ps, free = bank.take()
            for j in range(J):
                t = emit("pe", lambda e, j=j, ps=ps: e.transpose(
                    ps[0:DTR, j * P:(j + 1) * P], xdbl[p][:, j, 0:DTR], ident[:, :]), S["btr"], [xd, free])
            bank.free[i] = dr = emit("act", lambda e, ps=ps: e.activation(dtrT[0:DTR, :], ps[0:DTR, :], ACT.Copy),
                                     S["bev"], [t, last.get("dtrT_read"), memsets])
            Bv = xdbl[p][:, :, DTR:DTR + DS]
            t = emit("dve", lambda e: e.tensor_copy(bsp[:, :, 0:DS], Bv), S["bsp"], [xd, last.get("bsp_read")])
            t = emit("dve", lambda e: e.tensor_tensor(brem[:, :, :], Bv, bsp[:, :, 0:DS], ALU.subtract), S["bsp"], [t])
            yield 0.4
            for g in range(G):
                i, ps, free = bank.take()
                t2 = emit("pe", lambda e, g=g, ps=ps: e.matmul(ps[:, :], wdt_s[:, g * P:(g + 1) * P], dtrT[:, :],
                                                              start=True, stop=True), S["dtmm"], [dr, free])
                ta = emit("act", lambda e, g=g, ps=ps: e.activation(dt[p][:, g, :], ps[:, :], ACT.Abs), S["dta"],
                          [t2, last.get(("dt_read", p))])
                bank.free[i] = tb = emit("dve", lambda e, g=g, ps=ps: e.tensor_scalar(
                    xpad[:, g, 0:T], ps[:, :], 0.0, None, ALU.max), S["dtb"], [ta, last["conv_read"], pad_copied(c)])
                yield 0.9
            last["dtrT_read"] = t2
            t = emit("dve", lambda e: e.tensor_copy(bsp[:, :, DS:2 * DS], brem[:, :, :]), S["bsp"], [t])
            t = emit("dve", lambda e: e.tensor_tensor(bsp[:, :, 2 * DS:3 * DS], brem[:, :, :], bsp[:, :, DS:2 * DS],
                                                      ALU.subtract), S["bsp"], [t])
            for g in range(G):
                ta = emit("act", lambda e, g=g: e.activation(dt[p][:, g, :], dt[p][:, g, :], ACT.Exp, scale=-1.0),
                          S["dta"], [ta])
            for j in range(J):
                i, ps, free = bank.take()
                for g in range(G):
                    t3 = emit("pe", lambda e, g=g, j=j, ps=ps: e.matmul(
                        ps[:, g * P:(g + 1) * P], xs[p][:, g, j * P:(j + 1) * P], dskip[:, g, :], start=True, stop=True),
                        S["skip"], [xs_here, free, cst_diag])
                bank.free[i] = yi = emit("act", lambda e, j=j, ps=ps: e.activation(y[p][:, j, :], ps[:, :], ACT.Copy),
                                         S["yinit"], [t3, last.get(("y_read", p))])
                yield 0.9
            y_init[c] = yi
            for g in range(G):
                tb2 = emit("act", lambda e, g=g: e.activation(dt[p][:, g, :], dt[p][:, g, :], ACT.Ln, bias=1.0),
                           S["dta"], [ta])
            for g in range(G):
                td = emit("pool", lambda e, g=g: e.tensor_tensor(dt[p][:, g, :], dt[p][:, g, :], xpad[:, g, 0:T], ALU.add),
                          S["dtc"], [tb2, tb])
                yield 0.2
            last["relu_read"] = td
            dt_ready[c] = td
            for g in range(G):
                tu = emit("pool", lambda e, g=g: e.tensor_tensor(xs[p][:, g, :], xs[p][:, g, :], dt[p][:, g, :], ALU.mult),
                          S["u"], [td, t3])
                yield 0.2
            u_ready[c] = tu
            i, ps, free = bank.take()
            psb = ps[:, :].bitcast(BF16)
            for j in range(J):
                t2 = emit("pe", lambda e, j=j, psb=psb: e.transpose(
                    psb[0:SW, j * P:(j + 1) * P], bsp[:, j, :], identb[:, :]), S["btr"], [t, free])
            last["bsp_read"] = t2
            bank.free[i] = bT_ready[c] = emit("act", lambda e, psb=psb: e.activation(
                bT[p][:, :], psb[0:SW, 0:T], ACT.Copy), S["bev"], [t2, last.get(("bT_read", p))])
            yield 0.4
            r = S["rt"]
            t = emit("pool", lambda e: e.tensor_scalar(ginv[:, :], gss[:, :], 1e-24, 1.0, ALU.max, ALU.mult),
                     S["gq"], [tq, last.get("ginv")])
            last["gss"] = t
            t = emit("pool", lambda e: e.tensor_tensor(ginv[:, :], ginv[:, :], mhalf[:, :], ALU.pow), S["gq"], [t])
            t = emit("dve", lambda e: e.tensor_tensor(
                gl[:, :, :], glog[:, :, E:2 * E], ginv[:, :].unsqueeze(2).to_broadcast([P, J, E]), ALU.mult), r,
                [t, tl, last.get("gl")])
            last["ginv"] = t
            yield 0.1
            t = emit("dve", lambda e: e.tensor_tensor(gl[:, :, :], gl[:, :, :], glog[:, :, 0:E], ALU.add), r, [t])
            last["glog"] = t
            yield 0.1
            for j in range(J):
                t = emit("dve", lambda e, j=j: e.max(gtop[:, j, :], gl[:, j, :]), r, [t])
            yield 0.1
            t = emit("dve", lambda e: e.tensor_tensor(
                gmask[:, :, :], gl[:, :, :], gtop[:, :, 1:2].to_broadcast([P, J, E]), ALU.is_ge), r, [t])
            t = emit("dve", lambda e: e.tensor_tensor(
                gex[:, :, :], gl[:, :, :], gtop[:, :, 0:1].to_broadcast([P, J, E]), ALU.subtract), r, [t])
            last["gl"] = t
            yield 0.1
            t = emit("act", lambda e: e.activation(gex[:, :, :], gex[:, :, :], ACT.Exp), S["gx"], [t])
            yield 0.1
            t = emit("dve", lambda e: e.tensor_tensor(gex[:, :, :], gex[:, :, :], gmask[:, :, :], ALU.mult), r, [t])
            yield 0.1
            t = emit("dve", lambda e: e.tensor_reduce(gsum[:, :], gex[:, :, :], AX.X, ALU.add), r, [t])
            yield 0.1
            t = emit("dve", lambda e: e.reciprocal(gsum[:, :], gsum[:, :]), r, [t])
            yield 0.1
            t = emit("dve", lambda e: e.tensor_tensor(
                gate[b][:, :, :], gex[:, :, :], gsum[:, :].unsqueeze(2).to_broadcast([P, J, E]), ALU.mult), r,
                [t])
            gate_ready[c] = t
            yield 0.1
        def pad_copied(c):
            return None

        def affine(ln, ready):
            t = emit("pool", lambda e: e.tensor_tensor(h1[:, :, :], h1[:, :, :],
                                                       ln[:, 0:1, :].to_broadcast([P, J, DM]), ALU.mult),
                     S["aff"], [ready, w_rest])
            return emit("pool", lambda e: e.tensor_tensor(h1[:, :, :], h1[:, :, :],
                                                          ln[:, 1:2, :].to_broadcast([P, J, DM]), ALU.add), S["aff"], [t])

        def post(c):
            b, p = c % 3, c % 2
            y_done = last[("y_done", c)]
            for j in range(J):
                i, ps, free = bank.take()
                for k in range(K):
                    t = emit("pe", lambda e, k=k, j=j, ps=ps: e.matmul(
                        ps[:, :], xnT[b][:, k, j * P:(j + 1) * P], win_s[:, k, DI:2 * DI],
                        start=(k == 0), stop=(k == K - 1)), S["zmm"], [xnT_ready[c], free, cst_half])
                gi, gb, gfree = gbuf.take()
                tz = emit("act", lambda e, ps=ps, gb=gb: e.activation(gb[:, :], ps[:, :], ACT.Tanh), S["sz"], [t, gfree])
                bank.free[i] = tz = emit("dve", lambda e, ps=ps, gb=gb: e.scalar_tensor_tensor(
                    out=gb[:, :], in0=gb[:, :], scalar=1.0, in1=ps[:, :], op0=ALU.add, op1=ALU.mult), S["szm"], [tz])
                gbuf.free[gi] = ty = emit("pool", lambda e, j=j, gb=gb: e.tensor_tensor(
                    y[p][:, j, :], y[p][:, j, :], gb[:, :], ALU.mult), S["yz"], [tz, y_done])
                yield 1.7
                if j:
                    yield from gated_T(c, j - 1, ty_prev)
                ty_prev = ty
            yield from gated_T(c, J - 1, ty)
            yT_here = last["yT_w"]
            for j in range(J):
                for g in range(G):
                    t = emit("pe", lambda e, g=g, j=j: e.matmul(
                        acc[:, j, :], yT[:, g, j * P:(j + 1) * P], wout_s[:, g, :], start=(g == 0), stop=(g == G - 1)),
                        S["omm"], [yT_here, last.get("acc_read"), w_rest])
                yield 1.7
            last["yT_read"] = t
            for j in range(J):
                t2 = emit("dve", lambda e, j=j: e.tensor_tensor(h1[:, j, :], acc[:, j, :], xn[b][:, j, :], ALU.add),
                          S["hres"], [t, last.get("h1_out"), xn_ready[c]])
            last["acc_read"] = t2
            if c + 3 < NC:
                x_here[c + 3] = load_x(c + 3, [t2, last["xn_sq"]])
            yield 0.2
            yield from normalize("post", h1, 1e-12, [t2])
            ta = affine(ln1_s, last["post"])
            yield 0.1
            yield from transposed(h1, h1T, [ta], [last.get("h1T_read")], S["h1T"], S["ev"])
            h1T_here = last["tr"]
            last["h1_T"] = (S["h1T"], S["h1T"].count)
            for m in range(F):
                i, ps, free = bank.take()
                for k in range(K):
                    t = emit("pe", lambda e, k=k, m=m, ps=ps: e.matmul(
                        ps[:, :], f1_s[:, k, m * P:(m + 1) * P], h1T[:, k, :], start=(k == 0), stop=(k == K - 1)),
                        S["f1mm"], [h1T_here, free])
                bank.free[i] = tf = emit("act", lambda e, m=m, ps=ps: e.activation(
                    fT[:, m, :], ps[:, :], ACT.Identity, bias=fb1_s[:, m:m + 1]), S["f1a"], [t, last["yT_read"]])
                yield 1.0
                tf2 = emit("dve", lambda e, m=m: e.scalar_tensor_tensor(
                    out=fT[:, m, :], in0=fT[:, m, :], scalar=0.01, in1=fT[:, m, :], op0=ALU.mult, op1=ALU.max),
                    S["f1l"], [tf])
                yield 0.7
            f1_read = t
            tx = emit("sync", lambda e: e.dma_start(xres, x_c[c]), s_xres, [f1_read])
            for j in range(J):
                for m in range(F):
                    emit("pe", lambda e, m=m, j=j: e.matmul(
                        acc[:, j, :], fT[:, m, j * P:(j + 1) * P], f2_s[:, m, :], start=(m == 0), stop=False),
                        S["f2mm"], [tf2, last["acc_read"]])
                t = emit("pe", lambda e, j=j: e.matmul(acc[:, j, :], ones[:, :], fb2_s[:, :], start=False, stop=True),
                         S["f2mm"], [memsets])
                yield 2.1
            last["yT_read"] = t
            for j in range(J):
                t2 = emit("dve", lambda e, j=j: e.tensor_tensor(h1[:, j, :], h1[:, j, :], acc[:, j, :], ALU.add),
                          S["hres"], [t, ta, last["h1_T"]])
            last["acc_read"] = t2
            yield 0.2
            yield from normalize("post", h1, 1e-12, [t2])
            ta = affine(ln2_s, last["post"])
            ta = emit("pool", lambda e: e.tensor_tensor(h1[:, :, :], h1[:, :, :], xres, ALU.add), S["aff"], [ta, tx])
            last["h1T_read"] = ta
            yield 0.1

            r = S["rt"]
            t = emit("dve", lambda e: e.tensor_copy(gsp[:, :, 0:E], gate[b][:, :, :]), r, [gate_ready[c], last.get("gsp_read"), memsets])
            t = emit("dve", lambda e: e.tensor_tensor(grem[:, :, :], gate[b][:, :, :], gsp[:, :, 0:E], ALU.subtract), r, [t])
            yield 0.1
            t = emit("dve", lambda e: e.tensor_copy(gsp[:, :, DS:DS + E], grem[:, :, :]), r, [t])
            t = emit("dve", lambda e: e.tensor_tensor(gsp[:, :, 2 * DS:2 * DS + E], grem[:, :, :], gsp[:, :, DS:DS + E],
                                                      ALU.subtract), r, [t])
            yield 0.1
            i, ps, free = bank.take()
            psb = ps[:, :].bitcast(BF16)
            for j in range(J):
                t2 = emit("pe", lambda e, j=j, psb=psb: e.transpose(
                    psb[0:SW, j * P:(j + 1) * P], gsp[:, j, :], identb[:, :]), S["gtr"], [t, free])
            last["gsp_read"] = t2
            bank.free[i] = emit("act", lambda e, psb=psb: e.activation(
                gT[:, :], psb[0:SW, 0:T], ACT.Copy), S["gev"], [t2, last.get("gT_read")])
            yield 0.4
            i, ps, free = bank.take()
            for j in range(J):
                t2 = emit("pe", lambda e, j=j, ps=ps: e.transpose(
                    ps[0:E, j * P:(j + 1) * P], gate[b][:, j, :], ident[:, :]), S["gtr"], [gate_ready[c], free])
            bank.free[i] = gT_here = emit("act", lambda e, ps=ps: e.activation(
                gTf[:, :], ps[0:E, :], ACT.Copy), S["gev"], [t2, last.get("gT_read")])
            yield 0.4


            hid = [fT[:, m, :] for m in range(F)]
            hid_free = [last["yT_read"]] * F

            def hidden(pair):
                done = []
                for ex in pair:
                    i, ps, free = bank.take()
                    for k in range(K):
                        t = emit("pe", lambda e, k=k, ps=ps, ex=ex: e.matmul(
                            ps[:, :], m1_s[:, k, ex, :], xnT[b][:, k, :], start=(k == 0), stop=(k == K - 1)),
                            S["m1mm"], [xnT_ready[c], free, w_rest])
                    done.append((i, ps, t))
                last[("xnT", b)] = t
                for ex, (i, ps, t) in zip(pair, done):
                    bank.free[i] = te = emit("act", lambda e, ps=ps, ex=ex: e.activation(
                        hid[ex % F], ps[:, :], ACT.Gelu, bias=mb1_s[:, ex:ex + 1]), S["gelu"],
                        [t for _, _, t in done] + [hid_free[ex % F]])
                return te

            def gated(ex, te):
                i, ps, free = bank.take()
                t = emit("pe", lambda e, ps=ps: e.matmul(ps[:, :], sel[:, ex, :], gT[:, :], start=True, stop=True),
                         S["gbc"], [gT_here, free])
                bank.free[i] = tm = emit("dve", lambda e, ps=ps: e.tensor_tensor(
                    hid[ex % F], hid[ex % F], ps[:, :], ALU.mult), S["mg"], [te, t])
                return tm

            te = hidden((0, 1))
            yield 3.6
            for j in range(J):
                emit("pe", lambda e, j=j: e.matmul(
                    acc[:, j, :], gTf[:, j * P:(j + 1) * P], mb2_s[:, :], start=(j % 2 == 0), stop=False,
                    skip_group_check=True), S["m2mm"], [gT_here, last["acc_read"], w_rest])
            yield 1.7
            for ex in range(0, E, 2):
                te_next = hidden((ex + 2, ex + 3)) if ex + 2 < E else None
                yield 3.4
                tms = []
                for one in (ex, ex + 1):
                    tms.append(gated(one, te))
                    yield 0.2
                for one, tm in zip((ex, ex + 1), tms):
                    for j in range(J):
                        t = emit("pe", lambda e, j=j, one=one: e.matmul(
                            acc[:, j, :], hid[one % F][:, j * P:(j + 1) * P], m2_s[:, one, :], start=False,
                            stop=(one == E - 1), skip_group_check=True), S["m2mm"], [tm])
                    hid_free[one % F] = t
                    yield 1.7
                te = te_next
            last["gT_read"] = last["yT_read"] = t
            for j in range(J):
                t2 = emit("dve", lambda e, j=j: e.tensor_tensor(h1[:, j, :], h1[:, j, :], acc[:, j, :], ALU.add),
                          S["fin"], [t, ta])
            last["acc_read"] = t2
            last["h1_out"] = emit("sync", lambda e: e.dma_start(out_c[c], h1[:, :, :]), s_out, [t2])
            yield 0.2

        def gated_T(c, j, ty):
            p = c % 2
            i, ps, free = bank.take()
            for g in range(G):
                t = emit("pe", lambda e, g=g, ps=ps: e.transpose(
                    ps[:, g * P:(g + 1) * P], y[p][:, j, g * P:(g + 1) * P], ident[:, :]), S["ytr"], [ty, free])
            last[("y_read", p)] = t
            bank.free[i] = last["yT_w"] = emit("act", lambda e, ps=ps: e.activation(
                yT[:, :, j * P:(j + 1) * P], ps[:, :].rearrange("p (g t) -> p g t", g=G), ACT.Copy), S["yev"],
                [t, last.get("yT_read")])
            yield 0.45

        xn_ready, xnT_ready, gT_ready, bT_ready, dt_ready, u_ready, y_init, gate_ready = {}, {}, {}, {}, {}, {}, {}, {}

        bbc_here, bu_here, dA_here, scan_done, hT_done, sum_done = {}, {}, {}, {}, {}, {}
        x_here[2] = load_x(2)

        def spread_b(q):
            c, n = divmod(q, DS)
            i, ps, free = bank.take()
            t = emit("pe", lambda e: e.matmul(ps[:, :], sel[:, n, :], bT[c % 2][:, :], start=True, stop=True),
                     S["bbcmm"], [bT_ready[c], free])
            last[("bT_read", c % 2)] = t
            bi, bb, bfree = bbc.take()
            bank.free[i] = te = emit("act", lambda e: e.activation(bb[:, :], ps[:, :], ACT.Copy), S["bbc"], [t, bfree])
            bbc_here[q] = bi, bb, te

        def make_bu(w):
            q, half = divmod(w, G // 2)
            c = q // DS
            bi, bb, te = bbc_here[q]
            ri, rb, rfree = bu.take()
            t = emit("pool", lambda e: e.tensor_tensor(
                rb[:, :, :], xs[c % 2][:, 2 * half:2 * half + 2, :], bb[:, :].unsqueeze(1).to_broadcast([P, 2, T]),
                ALU.mult), S["bu"], [te, u_ready[c], rfree])
            bbc.free[bi] = t
            last[("u_read", c % 2)] = t
            bu_here[w] = ri, rb, t

        def make_dA(s):
            c, r = divmod(s, STEPS)
            n, g = divmod(r, G)
            ri, rb, rfree = dA.take()
            t = emit("act", lambda e: e.activation(rb[:, :], dt[c % 2][:, g, :], ACT.Exp, scale=nega[:, g, n:n + 1]),
                     S["dA"], [dt_ready[c], rfree, cst_neg])
            last[("dt_read", c % 2)] = t
            dA_here[s] = ri, rb, t

        def scan(s):
            c, r = divmod(s, STEPS)
            n, g = divmod(r, G)
            ai, ab, ta = dA_here.pop(s)
            wi, wb, tw = bu_here[s // 2]
            hi, hb, hfree = h.take()
            first = c % CPS == 0
            t = emit("dve", lambda e: e.tensor_tensor_scan(
                hb[:, :], ab[:, :], wb[:, s % 2, :], 0.0 if first else carry[:, n, g:g + 1], ALU.mult, ALU.add),
                S["scan"], [ta, tw, hfree, last.get("carry")])
            dA.free[ai] = bu.free[wi] = t
            if (c + 1) % CPS:
                last["carry"] = carry_wait[hi] = emit("pool", lambda e: e.tensor_copy(carry[:, n, g:g + 1], hb[:, T - 1:T]),
                                     S["carry"], [t])
            scan_done[s] = hi, hb, t

        def turn(s):
            g = s % G
            hi, hb, t = scan_done.pop(s)
            for j in range(J):
                t2 = emit("pe", lambda e, j=j: e.transpose(hT[j][:, g * P:(g + 1) * P], hb[:, j * P:(j + 1) * P],
                                                           ident[:, :]), S["hT"],
                          [t, sum_done.get((s // G - 1, j))])
            h.free[hi] = t2
            hT_done[s] = t2

        def add_up(q, j):
            c, n = divmod(q, DS)
            t = emit("dve", lambda e: e.scalar_tensor_tensor(
                out=y[c % 2][:, j, :], in0=hT[j][:, :], scalar=xdbl[c % 2][:, j, DTR + DS + n:DTR + DS + n + 1],
                in1=y[c % 2][:, j, :], op0=ALU.mult, op1=ALU.add), S["sum"],
                [hT_done[q * G + G - 1], y_init[c], sum_done.get((q - 1, j))])
            sum_done[(q, j)] = t
            last[("C_read", c % 2)] = t
            last[("y_done", c)] = t

        carry_wait = {}

        class Side:

            def __init__(self, gen, total):
                self.gen, self.total, self.done = gen, total, 0.0

            def upto(self, share):
                while self.gen is not None and (share >= 1 or self.done < share * self.total):
                    w = next(self.gen, None)
                    if w is None:
                        self.gen = None
                    else:
                        self.done += w

        PRE, POST = 51.0, 92.0
        for _ in pre(0):
            pass
        LB, LU, LA = 1, 2, 3
        for q in range(LB + 1):
            spread_b(q)
        for w in range(LU):
            make_bu(w)
        for s in range(LA):
            make_dA(s)
        total = NC * STEPS
        for c in range(NC):
            ahead = Side(pre(c + 1) if c + 1 < NC else None, PRE)
            behind = Side(post(c - 1) if c else None, POST)
            for r in range(STEPS):
                s = c * STEPS + r
                n, g = divmod(r, G)
                q = s // G
                ahead.upto((r + 1) / (STEPS - 12))
                if s + LA < total:
                    make_dA(s + LA)
                if s % 2 == 0 and s // 2 + LU < total // 2:
                    w = s // 2 + LU
                    make_bu(w)
                    if w % 2 == 1 and w // 2 + LB < NC * DS and w // 2 + LB not in bbc_here:
                        spread_b(w // 2 + LB)
                scan(s)
                if g == 0 and s:
                    turn(s - 1)
                    add_up(q - 1, 0)
                    add_up(q - 1, 1)
                if g == 1:
                    if s > G:
                        add_up(q - 1, 2)
                        add_up(q - 1, 3)
                if g == 2:
                    turn(s - 2)
                    turn(s - 1)
                if g == 3:
                    turn(s - 1)
                if c and r == G + 1:
                    pass
                behind_ready = not c or r >= 1
                if behind_ready:
                    behind.upto((r + 1) / STEPS)
        turn(total - 1)
        for j in range(J):
            add_up(NC * DS - 1, j)
        for _ in post(NC - 1):
            pass
        emit("sync", lambda e: e.nop() if hasattr(e, "nop") else e.wait_ge(s_out.sem, 16), None, [last["h1_out"]])

        block = ctx.enter_context(nc.Block())

        @block.sync
        def _(eng):
            for step in queue["sync"]:
                step(eng)

        @block.tensor
        def _(eng):
            for step in queue["pe"]:
                step(eng)

        @block.vector
        def _(eng):
            for step in queue["dve"]:
                step(eng)

        @block.scalar
        def _(eng):
            for step in queue["act"]:
                step(eng)

        @block.gpsimd
        def _(eng):
            for step in queue["pool"]:
                step(eng)


def kernel(**inputs):
    import concourse.bacc as bacc
    from concourse.bass_utils import run_bass_kernel_spmd

    a = {k: np.asarray(v) for k, v in inputs.items()}
    A, M = "L0_attn_", "L0_ffn_"

    def rows(w, p=P):
        return np.ascontiguousarray(w.reshape(-1, p, *w.shape[1:]).swapaxes(0, 1))

    def every(*vs):
        return np.ascontiguousarray(np.broadcast_to(np.stack(vs), (P, len(vs), vs[0].shape[0])))

    ds = a[A + "A_log"].shape[1]
    sel = np.zeros((3 * ds, ds, P), np.float32)
    for r in range(3 * ds):
        sel[r, r % ds, :] = 1.0
    bf = mybir.dt.np(BF16) if hasattr(mybir.dt, "np") else None
    if bf is None:
        import ml_dtypes
        bf = ml_dtypes.bfloat16
    arrays = {
        "x": a[A + "x"],
        "win": rows(a[A + "in_proj_w"].T),
        "wconv": rows(a[A + "conv_w"]),
        "bconv": rows(a[A + "conv_b"]),
        "wx": rows(a[A + "x_proj_w"].T),
        "wdt": np.concatenate([a[A + "dt_proj_w"].T, a[A + "dt_proj_b"][None]], 0),
        "alog": rows(a[A + "A_log"]),
        "dvec": rows(a[A + "D"]),
        "wout": rows(a[A + "out_proj_w"].T),
        "ln1": every(a[A + "ln1_w"], a[A + "ln1_b"]),
        "f1": rows(a[A + "ffn_w1"].T),
        "fb1": rows(a[A + "ffn_b1"]),
        "f2": rows(a[A + "ffn_w2"].T),
        "fb2": a[A + "ffn_b2"][None],
        "ln2": every(a[A + "ln2_w"], a[A + "ln2_b"]),
        "m1": np.ascontiguousarray(a[M + "w1"].reshape(a[M + "w1"].shape[0], -1, P, P).transpose(2, 1, 0, 3)),
        "mb1": np.ascontiguousarray(a[M + "b1"].T),
        "m2": np.ascontiguousarray(a[M + "w2"].transpose(1, 0, 2)),
        "mb2": a[M + "b2"],
        "cent": a[M + "centroids"],
        "wroute": rows(a[M + "w_route"].T),
        "ident": np.eye(P, dtype=np.float32),
        "identb": np.eye(P, dtype=np.float32).astype(bf),
        "sel": sel.astype(bf),
    }
    nc = bacc.Bacc("TRN2", target_bir_lowering=False, num_devices=1)
    arrays = {k: np.ascontiguousarray(v) for k, v in arrays.items()}
    args = [nc.dram_tensor(f"in_{k}", v.shape, mybir.dt.from_np(v.dtype), kind="ExternalInput").ap()
            for k, v in arrays.items()]
    out = nc.dram_tensor("out_y", a[A + "x"].shape, F32, kind="ExternalOutput").ap()
    build_block(nc, *args, out)
    r = run_bass_kernel_spmd(nc, [{f"in_{k}": v for k, v in arrays.items()}], core_ids=[0])
    return r.results[0]["out_y"]
```

```python
from contextlib import ExitStack

import numpy as np

import concourse.bass as bass
from concourse import mybir

F32 = mybir.dt.float32
BF16 = mybir.dt.bfloat16
ALU = mybir.AluOpType
ACT = mybir.ActivationFunctionType
AX = mybir.AxisListType

P = 128


COST = dict(
    x0=3., x1=3., x2=3., xres=3., out=3., m1w0=2.5, m1w1=2.5,
    tr=.11, inproj=.86, xproj=.06, btr=.11, dtmm=.86, skip=.21, gtr=.1, bbcmm=.21, hT=.11, zmm=.86, ytr=.11, omm=.43,
    h1T=.11, f1mm=.86, f2mm=.43, m1mm=.86, gbc=.21, m2mm=.43,
    ln_pre=.3, ln_post=.3, rt=.12, conv=.6, silm=.6, xdbl=.3, bsp=.1, dtb=.6, scan=.64, sum=.66, szm=.6, hres=.6,
    f1l=.6, mg=.6, fin=.6,
    ev=.48, xpad=.48, silu=.5, bev=.48, dta=.5, yinit=.48, gq=.2, gn=.5, gx=.1, gev=.48, bbc=.48, dA=.61, sz=.48, yev=.48,
    f1a=.48, m1ev=.48, gelu=1.1,
    rs_pre=.6, rs_post=.6, dtc=1.22, u=1.22, bu=2.3, carry=.13, yz=1.22, aff=1.22, pad=.1)


class Stage:

    def __init__(self, sem, step=1, cost=.1):
        self.sem, self.step, self.count, self.cost, self.end = sem, step, 0, cost, {0: 0.0}


class Ring:

    def __init__(self, bufs):
        self.bufs, self.free, self.open, self.turn = bufs, [None] * len(bufs), [False] * len(bufs), -1

    def take(self):
        for _ in self.bufs:
            self.turn = (self.turn + 1) % len(self.bufs)
            if not self.open[self.turn]:
                break
        i = self.turn
        assert not self.open[i]
        self.open[i] = True
        return i, self.bufs[i], self.free[i]

    def give(self, i, mark):
        self.free[i], self.open[i] = mark, False
        return mark


def build_block(nc: bass.Bass, x, win, wconv, bconv, wx, wdt, alog, dvec, wout, ln1, f1, fb1, f2, fb2,
                ln2, m1, mb1, m2, mb2, cent, wroute, ident_in, identb_in, sel_in, out):
    B, L, DM = x.shape
    K = DM // P
    DI = win.shape[2] // 2
    G = DI // P
    DC = wconv.shape[2]
    DTR = wdt.shape[0] - 1
    DS = alog.shape[2]
    XW = DTR + 2 * DS
    F = f1.shape[2] // P
    E = m1.shape[0]
    SW = 3 * DS
    T = 512
    J = T // P
    NC = B * L // T
    CPS = L // T
    STEPS = DS * G

    x_c = x.rearrange("b (h j p) d -> (b h) p j d", j=J, p=P)
    out_c = out.rearrange("b (h j p) d -> (b h) p j d", j=J, p=P)

    ctx = ExitStack()
    with ctx:
        def sb(name, shape, dt=F32):
            return ctx.enter_context(nc.sbuf_tensor(name, shape, dt))

        def stage(name, step=1):
            return Stage(ctx.enter_context(nc.semaphore("s_" + name)), step, COST.get(name, .1))

        win_s = sb("win_s", [P, K, 2 * DI])
        wconv_s = sb("wconv_s", [P, G, DC])
        bconv_s = sb("bconv_s", [P, G])
        wx_s = sb("wx_s", [P, G, XW])
        wdt_s = sb("wdt_s", [DTR + 1, DI])
        alog_s = sb("alog_s", [P, G, DS])
        nega = sb("nega", [P, G, DS])
        d_s = sb("d_s", [P, G])
        wout_s = sb("wout_s", [P, G, DM])
        ln1_s = sb("ln1_s", [P, 2, DM])
        ln2_s = sb("ln2_s", [P, 2, DM])
        f1_s = sb("f1_s", [P, K, F * P])
        fb1_s = sb("fb1_s", [P, F])
        f2_s = sb("f2_s", [P, F, DM])
        fb2_s = sb("fb2_s", [1, DM])
        mb1_s = sb("mb1_s", [P, E])
        mb2_s = sb("mb2_s", [E, DM])
        wrc_s = sb("wrc_s", [P, K, 2 * E])
        ident = sb("ident", [P, P])
        identb = sb("identb", [P, P], BF16)
        sel = sb("sel", [SW, DS, P], BF16)
        ones = sb("ones", [1, P])
        mhalf = sb("mhalf", [P, J])
        dskip = sb("dskip", [P, G, P])
        css = sb("css", [E, 2])

        xn = [sb(f"xn{i}", [P, J, DM]) for i in range(3)]
        xnT = [sb(f"xnT{i}", [P, K, T]) for i in range(3)]
        xpad = sb("xpad", [P, G, T + DC - 1])
        xs = [sb(f"xs{i}", [P, G, T]) for i in range(2)]
        dt = [sb(f"dt{i}", [P, G, T]) for i in range(2)]
        y = [sb(f"y{i}", [P, J, DI]) for i in range(2)]
        xdbl = [sb(f"xdbl{i}", [P, J, XW]) for i in range(2)]
        bT = [sb(f"bT{i}", [SW, T], BF16) for i in range(2)]
        bsp = sb("bsp", [P, J, SW], BF16)
        brem = sb("brem", [P, J, DS])
        dtrT = sb("dtrT", [DTR + 1, T])
        yT = sb("yT", [P, G, T])
        fT = yT
        h1 = sb("hres", [P, J, DM])
        cent_s = h1[0:E, 0, :]
        h1T = sb("hresT", [P, K, T])
        xres = sb("xres", [P, J, DM])
        junk = sb("junk", [P, DM], BF16)
        gss = [sb(f"gss{i}", [P, J]) for i in range(2)]
        ginv = sb("ginv", [P, J])
        glog = [sb(f"glog{i}", [P, J, 2 * E]) for i in range(2)]
        gl = sb("gl", [P, J, E])
        gtop = sb("gtop", [P, J, 8])
        gmask = sb("gmask", [P, J, E])
        gex = sb("gex", [P, J, E])
        gsum = sb("gsum", [P, J])
        gate = sb("gate", [P, J, E])
        grem = sb("grem", [P, J, E])
        gsp = sb("gsp", [P, J, SW], BF16)
        gT = sb("gT", [SW, T], BF16)
        small = {k: (sb(f"{k}_st", [P, J, 6]), sb(f"{k}_mv", [P, J, 2]), sb(f"{k}_ve", [P, J]), sb(f"{k}_rs", [P, J]))
                 for k in ("pre", "post")}
        carry = sb("carry", [P, DS, G])

        NDA, NH, NBU = 4, 8, 3
        dA = Ring([sb(f"dA{i}", [P, T]) for i in range(NDA)])
        hrows = sb("hrows", [P, NH, T])
        h = Ring([hrows[:, i, :] for i in range(NH)])
        bu = Ring([sb(f"bu{i}", [P, 2, T]) for i in range(NBU)])
        bbc = Ring([sb(f"bbc{i}", [P, T]) for i in range(2)])
        gbuf = Ring([sb(f"gbuf{i}", [P, T]) for i in range(2)])

        m1w = Ring([sb(f"m1w{i}", [P, K, P]) for i in range(2)])
        m2w = Ring([sb(f"m2w{i}", [P, DM]) for i in range(5)])
        hid = Ring([sb(f"hid{i}", [P, T]) for i in range(4)])

        hT = Ring([ctx.enter_context(nc.psum_tensor(f"hT{i}", [P, DI], F32)) for i in range(3)])
        acc = ctx.enter_context(nc.psum_tensor("acc", [P, J, DM], F32))
        bank = Ring([ctx.enter_context(nc.psum_tensor(f"bank{i}", [P, T], F32)) for i in range(3)])

        queue = {k: [] for k in ("sync", "pe", "dve", "act", "pool")}
        waited = {k: {} for k in queue}
        clock = dict.fromkeys(queue, 0.0)
        hurry = []
        newest = [0.0]

        def emit(eng, make, done=None, after=()):
            start = clock[eng]
            for mark in after:
                if mark is None:
                    continue
                st, n = mark
                start = max(start, st.end[n] + .13)
                if waited[eng].get(st, 0) < n:
                    waited[eng][st] = n
                    queue[eng].append(lambda e, s=st.sem, n=n: e.wait_ge(s, n))
            clock[eng] = newest[0] = start + (done.cost if done else .43)
            if done is None:
                queue[eng].append(make)
                return None
            done.count += done.step
            done.end[done.count] = clock[eng]
            queue[eng].append(lambda e, s=done: make(e).then_inc(s.sem, s.step))
            return done, done.count

        s_wfirst, s_wrest = stage("wfirst", 16), stage("wrest", 16)
        s_x = [stage(f"x{i}", 16) for i in range(3)]
        s_m1, s_m2 = [stage(f"m1w{i}", 16) for i in range(2)], [stage(f"m2w{i}", 16) for i in range(5)]
        s_xres, s_out = stage("xres", 16), stage("out", 16)

        def load_x(c, after=()):
            return emit("sync", lambda e: e.dma_start(xn[c % 3][:, :, :], x_c[c]), s_x[c % 3], after)

        x_here = {0: load_x(0)}
        for dst, src in ((ident[:, :], ident_in), (win_s[:, :, :], win), (wconv_s[:, :, :], wconv),
                         (bconv_s[:, :], bconv), (d_s[:, :], dvec), (alog_s[:, :, :], alog),
                         (wx_s[:, :, :], wx), (wdt_s[:, :], wdt), (cent_s, cent),
                         (wrc_s[:, :, 0:E], wroute), (identb[:, :], identb_in), (sel[:, :, :], sel_in)):
            w_first = emit("sync", lambda e, d=dst, s=src: e.dma_start(d, s), s_wfirst)
        x_here[1] = load_x(1)
        for dst, src in ((mb1_s[:, :], mb1), (mb2_s[:, :], mb2),
                         (wout_s[:, :, :], wout), (ln1_s[:, :, :], ln1), (f1_s[:, :, :], f1), (fb1_s[:, :], fb1),
                         (f2_s[:, :, :], f2), (fb2_s[:, :], fb2), (ln2_s[:, :, :], ln2)):
            w_rest = emit("sync", lambda e, d=dst, s=src: e.dma_start(d, s), s_wrest)

        s_ms, s_cst, s_neg, s_css = stage("ms"), stage("cst"), stage("neg"), stage("css")
        emit("pool", lambda e: e.memset(mhalf[:, :], -0.5), s_ms)
        emit("pool", lambda e: e.memset(dtrT[:, :], 1.0), s_ms)
        emit("pool", lambda e: e.memset(gsp[:, :, :], 0.0), s_ms)
        memsets = emit("pool", lambda e: e.memset(ones[:, :], 1.0), s_ms)

        t = emit("act", lambda e: e.activation(nega[:, :, :], alog_s[:, :, :], ACT.Exp), s_neg, [w_first])
        css_sq = emit("act", lambda e: e.activation(junk[0:E, :], cent_s, ACT.Square, accum_out=css[:, 0:1]),
                      s_css, [w_first])
        cst_neg = emit("dve", lambda e: e.tensor_scalar(nega[:, :, :], nega[:, :, :], -1.0, None, ALU.mult),
                       s_cst, [t])
        for buf in (wconv_s[:, :, :], bconv_s[:, :], win_s[:, :, DI:2 * DI]):
            cst_half = emit("dve", lambda e, b=buf: e.tensor_scalar(b, b, 0.5, None, ALU.mult), s_cst, [w_first])
        for g in range(G):
            cst_diag = emit("dve", lambda e, g=g: e.tensor_scalar(dskip[:, g, :], ident[:, :], d_s[:, g:g + 1],
                                                                  None, ALU.mult), s_cst, [w_first])
        t = emit("pool", lambda e: e.tensor_scalar(css[:, 1:2], css[:, 0:1], 1e-24, 1.0, ALU.max, ALU.mult),
                 s_css, [css_sq])
        t = emit("pool", lambda e: e.tensor_tensor(css[:, 0:1], css[:, 1:2], mhalf[0:E, 0:1], ALU.pow),
                 s_css, [t, memsets])
        t = emit("dve", lambda e: e.tensor_scalar(cent_s, cent_s, css[:, 0:1], None, ALU.mult),
                 s_cst, [t])
        i, ps, free = bank.take()
        for k in range(K):
            t2 = emit("pe", lambda e, k=k, ps=ps: e.transpose(ps[:, k * E:(k + 1) * E], cent_s[:, k * P:(k + 1) * P],
                                                              ident[0:E, 0:E]), s_css, [t, w_first])
        cst_cent = emit("dve", lambda e, ps=ps: e.tensor_copy(
            wrc_s[:, :, E:2 * E], ps[:, 0:K * E].rearrange("p (k e) -> p k e", k=K)), s_cst, [t2])
        bank.give(i, cst_cent)

        S = {n: stage(n) for n in (
            "ln_pre", "ln_post", "rs_pre", "rs_post", "tr", "ev", "inproj", "pad", "xpad", "conv", "silu", "silm",
            "xproj", "xdbl", "bsp", "btr", "bev", "dtmm", "dta", "dtb", "dtc", "u", "skip", "yinit",
            "gq", "gn", "rt", "gate", "gx", "gtr", "gev",
            "bbcmm", "bbc", "bu", "dA", "scan", "carry", "hT", "sum",
            "zmm", "sz", "szm", "yz", "ytr", "yev", "omm", "hres", "aff", "h1T", "f1mm", "f1a", "f1l", "f2mm",
            "m1mm", "m1ev", "gelu", "gbc", "mg", "m2mm", "fin")}
        last = {}

        def until(queued):
            while not queued():
                yield -1.0

        def there(mark):
            while mark[0].end[mark[1]] > clock["dve"] and not hurry:
                yield -.5

        def idle(eng):
            while clock[eng] > clock["dve"] + LAG and not hurry:
                yield -.5

        def some(ring):
            while sum(ring.open) >= len(ring.bufs) - (ring is bank):
                yield -.3
            return ring.take()

        def normalize(tag, buf, eps, ready):
            st, mv, ve, rs = small[tag]
            lnS, rsS = S["ln_" + tag], S["rs_" + tag]
            for j in range(J):
                t = emit("dve", lambda e, j=j: e.bn_stats(st[:, j, :], buf[:, j, :]), lnS, ready + [last.get(tag)])
                if j % 2:
                    yield 0
            for j in range(J):
                t2 = emit("dve", lambda e, j=j: e.bn_aggr(mv[:, j, :], st[:, j, :]), lnS, [t])
            yield 0
            t = emit("pool", lambda e: e.tensor_scalar(ve[:, :], mv[:, :, 1], eps, 1.0, ALU.add, ALU.mult), rsS, [t2])
            t = emit("pool", lambda e: e.tensor_tensor(rs[:, :], ve[:, :], mhalf[:, :], ALU.pow), rsS, [t, memsets])
            yield 0
            yield 0
            for j in range(J):
                t2 = emit("dve", lambda e, j=j: e.tensor_scalar(buf[:, j, :], buf[:, j, :], mv[:, j, 0:1], rs[:, j:j + 1],
                                                                ALU.subtract, ALU.mult), lnS, [t])
                if j % 2:
                    yield 0
            last[tag] = t2

        def transposed(src, dst, ready, free_dst, pe_done, ev_done):
            yield 0
            for k in range(K):
                i, ps, free = yield from some(bank)
                for j in range(J):
                    t = emit("pe", lambda e, k=k, j=j, ps=ps: e.transpose(
                        ps[:, j * P:(j + 1) * P], src[:, j, k * P:(k + 1) * P], ident[:, :]), pe_done, ready + [free, w_first])
                yield 0
                bank.give(i, emit("act", lambda e, k=k, ps=ps: e.activation(dst[:, k, :], ps[:, :], ACT.Copy),
                                    ev_done, [t] + free_dst))
                yield 0.45
            last["tr"] = bank.free[i]

        def pre(c):
            b, p = c % 3, c % 2
            yield from until(lambda: c in x_here)
            yield from normalize("pre", xn[b], 1e-5, [x_here[c]])
            xn_here = last["pre"]
            xn_ready[c] = xn_here
            yield from until(lambda: c < 3 or (c - 3 in gated and c - 3 in moe_done))
            yield from transposed(xn[b], xnT[b], [xn_here], [last.get(("xnT", b))], S["tr"], S["ev"])
            xnT_here = last["tr"]
            xnT_ready[c] = xnT_here
            yield from until(lambda: c < 2 or c - 2 in routed)
            for j in range(J):
                tq = emit("act", lambda e, j=j: e.activation(junk[:, :], xn[b][:, j, :], ACT.Square,
                                                             accum_out=gss[p][:, j:j + 1]), S["gq"],
                          [xn_here, last.get(("gss", p)), last.get("junk")])
                last["junk"] = tq
            i, ps, free = yield from some(bank)
            for j in range(J):
                for k in range(K):
                    t = emit("pe", lambda e, k=k, j=j, ps=ps: e.matmul(
                        ps[:, j * 2 * E:(j + 1) * 2 * E], xnT[b][:, k, j * P:(j + 1) * P], wrc_s[:, k, :],
                        start=(k == 0), stop=(k == K - 1)), S["gtr"], [xnT_here, free, cst_cent])
            yield 0
            tl = bank.give(i, emit("dve", lambda e, ps=ps: e.tensor_copy(
                glog[p][:, :, :], ps[:, 0:J * 2 * E].rearrange("p (j e) -> p j e", j=J)), S["rt"], [t, last.get(("glog", p))]))
            last["xn_sq"] = sq_ready[c] = tq
            glog_ready[c] = tl
            yield 1.7
            tp = last.get("conv_read")
            if c % CPS:
                pad = emit("pool", lambda e: e.tensor_copy(xpad[:, :, 0:DC - 1], xpad[:, :, T:T + DC - 1]), S["pad"],
                           [tp, last.get("xpad_w")])
            else:
                pad = emit("pool", lambda e: e.memset(xpad[:, :, 0:DC - 1], 0.0), S["pad"], [tp])
            for g in range(G):
                i, ps, free = yield from some(bank)
                for k in range(K):
                    t = emit("pe", lambda e, g=g, k=k, ps=ps: e.matmul(
                        ps[:, :], win_s[:, k, g * P:(g + 1) * P], xnT[b][:, k, :],
                        start=(k == 0), stop=(k == K - 1)), S["inproj"], [xnT_here, free])
                    yield 0.86
                yield 0
                xw = bank.give(i, emit("act", lambda e, g=g, ps=ps: e.activation(
                    xpad[:, g, DC - 1:], ps[:, :], ACT.Copy), S["xpad"], [t, tp, pad, last.get("relu_read")]))
            last["xpad_w"] = xw
            for g in range(0, G, 2):
                two = (g, g + 1)
                taps = {}
                for gg in two:
                    taps[gg] = emit("act", lambda e, g=gg: e.activation(
                        xs[p][:, g, :], xpad[:, g, DC - 1:], ACT.Identity, bias=bconv_s[:, g:g + 1],
                        scale=wconv_s[:, g, DC - 1:DC]), S["silu"], [xw, last.get(("u_read", p)), cst_half])
                yield 0
                for k in range(DC - 1):
                    for gg in two:
                        taps[gg] = emit("dve", lambda e, g=gg, k=k: e.scalar_tensor_tensor(
                            out=xs[p][:, g, :], in0=xpad[:, g, k:k + T], scalar=wconv_s[:, g, k:k + 1],
                            in1=xs[p][:, g, :], op0=ALU.mult, op1=ALU.add), S["conv"], [taps[gg], pad])
                    yield 1.2
                    yield 0
                last["conv_read"] = taps[g + 1]
                gates = {}
                for gg in two:
                    gi, gb, gfree = yield from some(gbuf)
                    gates[gg] = gi, gb, emit("act", lambda e, g=gg, gb=gb: e.activation(
                        gb[:, :], xs[p][:, g, :], ACT.Tanh), S["silu"], [taps[g + 1], gfree])
                yield 0
                for gg in two:
                    gi, gb, ta = gates[gg]
                    xs_here = gbuf.give(gi, emit("dve", lambda e, g=gg, gb=gb: e.scalar_tensor_tensor(
                        out=xs[p][:, g, :], in0=gb[:, :], scalar=1.0, in1=xs[p][:, g, :], op0=ALU.add, op1=ALU.mult),
                        S["silm"], [ta]))
                yield 1.2
            yield 0
            i, ps, free = yield from some(bank)
            for j in range(J):
                for g in range(G):
                    t = emit("pe", lambda e, g=g, j=j, ps=ps: e.matmul(
                        ps[:, j * XW:(j + 1) * XW], xs[p][:, g, j * P:(j + 1) * P], wx_s[:, g, :],
                        start=(g == 0), stop=(g == G - 1)), S["xproj"], [xs_here, free])
                yield 0.86
            yield 0
            xd = bank.give(i, emit("dve", lambda e, ps=ps: e.tensor_copy(
                xdbl[p][:, :, :], ps[:, 0:J * XW].rearrange("p (j e) -> p j e", j=J)), S["xdbl"],
                [t, last.get(("C_read", p))]))
            yield 1.0
            i, ps, free = yield from some(bank)
            for j in range(J):
                t = emit("pe", lambda e, j=j, ps=ps: e.transpose(
                    ps[0:DTR, j * P:(j + 1) * P], xdbl[p][:, j, 0:DTR], ident[:, :]), S["btr"], [xd, free])
            yield 0
            dr = bank.give(i, emit("act", lambda e, ps=ps: e.activation(dtrT[0:DTR, :], ps[0:DTR, :], ACT.Copy),
                                     S["bev"], [t, last.get("dtrT_read"), memsets]))
            Bv = xdbl[p][:, :, DTR:DTR + DS]
            t = emit("dve", lambda e: e.tensor_copy(bsp[:, :, 0:DS], Bv), S["bsp"], [xd, last.get("bsp_read")])
            t = emit("dve", lambda e: e.tensor_tensor(brem[:, :, :], Bv, bsp[:, :, 0:DS], ALU.subtract), S["bsp"], [t])
            yield 0.4
            for g in range(G):
                i, ps, free = yield from some(bank)
                t2 = emit("pe", lambda e, g=g, ps=ps: e.matmul(ps[:, :], wdt_s[:, g * P:(g + 1) * P], dtrT[:, :],
                                                              start=True, stop=True), S["dtmm"], [dr, free])
                yield 0
                ta = emit("act", lambda e, g=g, ps=ps: e.activation(dt[p][:, g, :], ps[:, :], ACT.Abs), S["dta"],
                          [t2, last.get(("dt_read", p))])
                tb = bank.give(i, emit("dve", lambda e, g=g, ps=ps: e.tensor_scalar(
                    xpad[:, g, 0:T], ps[:, :], 0.0, None, ALU.max), S["dtb"], [ta, last["conv_read"]]))
                yield 0.9
            last["dtrT_read"] = t2
            t = emit("dve", lambda e: e.tensor_copy(bsp[:, :, DS:2 * DS], brem[:, :, :]), S["bsp"], [t])
            t = emit("dve", lambda e: e.tensor_tensor(bsp[:, :, 2 * DS:3 * DS], brem[:, :, :], bsp[:, :, DS:2 * DS],
                                                      ALU.subtract), S["bsp"], [t])
            for g in range(G):
                ta = emit("act", lambda e, g=g: e.activation(dt[p][:, g, :], dt[p][:, g, :], ACT.Exp, scale=-1.0),
                          S["dta"], [ta])
            yield from until(lambda: c < 2 or c - 2 in gated)
            for j in range(J):
                i, ps, free = yield from some(bank)
                for g in range(G):
                    t3 = emit("pe", lambda e, g=g, j=j, ps=ps: e.matmul(
                        ps[:, g * P:(g + 1) * P], xs[p][:, g, j * P:(j + 1) * P], dskip[:, g, :], start=True, stop=True),
                        S["skip"], [xs_here, free, cst_diag])
                yield 0
                yi = bank.give(i, emit("act", lambda e, j=j, ps=ps: e.activation(y[p][:, j, :], ps[:, :], ACT.Copy),
                                         S["yinit"], [t3, last.get(("y_read", p))]))
                yield 0.9
            y_init[c] = yi
            for g in range(G):
                tb2 = emit("act", lambda e, g=g: e.activation(dt[p][:, g, :], dt[p][:, g, :], ACT.Ln, bias=1.0),
                           S["dta"], [ta])
            for g in range(G):
                yield from idle("pool")
                td = emit("pool", lambda e, g=g: e.tensor_tensor(dt[p][:, g, :], dt[p][:, g, :], xpad[:, g, 0:T], ALU.add),
                          S["dtc"], [tb2, tb])
                yield 1.0
            last["relu_read"] = td
            dt_ready[c] = td
            for g in range(G):
                yield from idle("pool")
                tu = emit("pool", lambda e, g=g: e.tensor_tensor(xs[p][:, g, :], xs[p][:, g, :], dt[p][:, g, :], ALU.mult),
                          S["u"], [td, t3])
                yield 1.0
            u_ready[c] = tu
            i, ps, free = yield from some(bank)
            psb = ps[:, :].bitcast(BF16)
            for j in range(J):
                t2 = emit("pe", lambda e, j=j, psb=psb: e.transpose(
                    psb[0:SW, j * P:(j + 1) * P], bsp[:, j, :], identb[:, :]), S["btr"], [t, free])
            last["bsp_read"] = t2
            yield 0
            bT_ready[c] = bank.give(i, emit("act", lambda e, psb=psb: e.activation(
                bT[p][:, :], psb[0:SW, 0:T], ACT.Copy), S["bev"], [t2, last.get(("bT_read", p))]))
            yield 0.4

        def route(c):
            tq, tl = sq_ready[c], glog_ready[c]
            r = S["rt"]
            t = emit("pool", lambda e: e.tensor_scalar(ginv[:, :], gss[c % 2][:, :], 1e-24, 1.0, ALU.max, ALU.mult),
                     S["gn"], [tq, last.get("ginv")])
            last["gss", c % 2] = t
            t = emit("pool", lambda e: e.tensor_tensor(ginv[:, :], ginv[:, :], mhalf[:, :], ALU.pow), S["gn"], [t])
            yield 0
            yield 0
            t = emit("dve", lambda e: e.tensor_tensor(
                gl[:, :, :], glog[c % 2][:, :, E:2 * E], ginv[:, :].unsqueeze(2).to_broadcast([P, J, E]), ALU.mult), r,
                [t, tl, last.get("gl")])
            last["ginv"] = t
            yield 0
            t = emit("dve", lambda e: e.tensor_tensor(gl[:, :, :], gl[:, :, :], glog[c % 2][:, :, 0:E], ALU.add), r, [t])
            last["glog", c % 2] = t
            yield 0
            tgl = t
            for j in range(J):
                t = emit("dve", lambda e, j=j: e.max(gtop[:, j, :], gl[:, j, :]), r, [tgl])
            yield 0
            t = emit("dve", lambda e: e.tensor_tensor(
                gmask[:, :, :], gl[:, :, :], gtop[:, :, 1:2].to_broadcast([P, J, E]), ALU.is_ge), r, [t])
            t = emit("dve", lambda e: e.tensor_tensor(
                gex[:, :, :], gl[:, :, :], gtop[:, :, 0:1].to_broadcast([P, J, E]), ALU.subtract), r, [t])
            last["gl"] = t
            yield 0
            t = emit("act", lambda e: e.activation(gex[:, :, :], gex[:, :, :], ACT.Exp), S["gx"], [t])
            yield 0
            t = emit("dve", lambda e: e.tensor_tensor(gex[:, :, :], gex[:, :, :], gmask[:, :, :], ALU.mult), r, [t])
            yield 0
            t = emit("dve", lambda e: e.tensor_reduce(gsum[:, :], gex[:, :, :], AX.X, ALU.add), r, [t])
            yield 0
            t = emit("dve", lambda e: e.reciprocal(gsum[:, :], gsum[:, :]), r, [t])
            yield 0
            t = emit("dve", lambda e: e.tensor_tensor(
                gate[:, :, :], gex[:, :, :], gsum[:, :].unsqueeze(2).to_broadcast([P, J, E]), ALU.mult), r,
                [t, last.get("gate_read")])
            routed.add(c)
            return t


        def affine(ln, ready):
            H = J // 2
            for r in (0, H):
                yield from idle("pool")
                t = emit("pool", lambda e, r=r: e.tensor_tensor(
                    h1[:, r:r + H, :], h1[:, r:r + H, :], ln[:, 0:1, :].to_broadcast([P, H, DM]), ALU.mult),
                    S["aff"], [ready, w_rest])
            for r in (0, H):
                yield from idle("pool")
                t2 = emit("pool", lambda e, r=r: e.tensor_tensor(
                    h1[:, r:r + H, :], h1[:, r:r + H, :], ln[:, 1:2, :].to_broadcast([P, H, DM]), ALU.add),
                    S["aff"], [t])
            last["aff"] = t2
            yield 0

        def attn(c):
            b, p = c % 3, c % 2
            yield from until(lambda: c in summed)
            y_done = last[("y_done", c)]
            for j in range(J):
                i, ps, free = yield from some(bank)
                for k in range(K):
                    t = emit("pe", lambda e, k=k, j=j, ps=ps: e.matmul(
                        ps[:, :], xnT[b][:, k, j * P:(j + 1) * P], win_s[:, k, DI:2 * DI],
                        start=(k == 0), stop=(k == K - 1)), S["zmm"], [xnT_ready[c], free, cst_half])
                    yield 0.86
                yield 0
                gi, gb, gfree = yield from some(gbuf)
                tz = emit("act", lambda e, ps=ps, gb=gb: e.activation(gb[:, :], ps[:, :], ACT.Tanh), S["sz"], [t, gfree])
                yield 0
                tz = bank.give(i, emit("dve", lambda e, ps=ps, gb=gb: e.scalar_tensor_tensor(
                    out=gb[:, :], in0=gb[:, :], scalar=1.0, in1=ps[:, :], op0=ALU.add, op1=ALU.mult), S["szm"], [tz]))
                yield 0
                yield from idle("pool")
                ty = gbuf.give(gi, emit("pool", lambda e, j=j, gb=gb: e.tensor_tensor(
                    y[p][:, j, :], y[p][:, j, :], gb[:, :], ALU.mult), S["yz"], [tz, y_done]))
                if j:
                    yield from gated_T(c, j - 1, ty_prev)
                ty_prev = ty
            yield from gated_T(c, J - 1, ty)
            yT_here = last["yT_w"]
            gated.add(c)
            for r in range(0, J, 2):
                i, ps, free = yield from some(bank)
                for j in (r, r + 1):
                    for g in range(G):
                        t = emit("pe", lambda e, g=g, j=j, ps=ps: e.matmul(
                            ps[:, j % 2 * DM:(j % 2 + 1) * DM], yT[:, g, j * P:(j + 1) * P], wout_s[:, g, :],
                            start=(g == 0), stop=(g == G - 1)), S["omm"], [yT_here, free, w_rest])
                        yield 0.43
                yield 0
                t2 = bank.give(i, emit("dve", lambda e, r=r, ps=ps: e.tensor_tensor(
                    h1[:, r:r + 2, :], ps[:, :].rearrange("p (j d) -> p j d", j=2), xn[b][:, r:r + 2, :], ALU.add),
                    S["hres"], [t, last.get("h1_out"), xn_ready[c]]))
            last["yT_read"] = t
            if c + 3 < NC:
                x_here[c + 3] = load_x(c + 3, [t2, last["xn_sq"]])
            yield 0.2
            yield from normalize("post", h1, 1e-12, [t2])
            yield from affine(ln1_s, last["post"])
            ta = last["aff"]
            yield from transposed(h1, h1T, [ta], [last.get("h1T_read")], S["h1T"], S["ev"])
            h1T_here = last["tr"]
            last["h1_T"] = (S["h1T"], S["h1T"].count)
            for m in range(F):
                i, ps, free = yield from some(bank)
                for k in range(K):
                    t = emit("pe", lambda e, k=k, m=m, ps=ps: e.matmul(
                        ps[:, :], f1_s[:, k, m * P:(m + 1) * P], h1T[:, k, :], start=(k == 0), stop=(k == K - 1)),
                        S["f1mm"], [h1T_here, free])
                    yield 0.86
                yield 0
                tf = bank.give(i, emit("act", lambda e, m=m, ps=ps: e.activation(
                    fT[:, m, :], ps[:, :], ACT.Identity, bias=fb1_s[:, m:m + 1]), S["f1a"], [t, last["yT_read"]]))
                yield 0
                tf2 = emit("dve", lambda e, m=m: e.scalar_tensor_tensor(
                    out=fT[:, m, :], in0=fT[:, m, :], scalar=0.01, in1=fT[:, m, :], op0=ALU.mult, op1=ALU.max),
                    S["f1l"], [tf])
            last["h1T_read"] = t
            for r in range(0, J, 2):
                i, ps, free = yield from some(bank)
                for j in (r, r + 1):
                    for m in range(F):
                        emit("pe", lambda e, m=m, j=j, ps=ps: e.matmul(
                            ps[:, j % 2 * DM:(j % 2 + 1) * DM], fT[:, m, j * P:(j + 1) * P], f2_s[:, m, :],
                            start=(m == 0), stop=False), S["f2mm"], [tf2, free])
                        yield 0.43
                    t = emit("pe", lambda e, j=j, ps=ps: e.matmul(
                        ps[:, j % 2 * DM:(j % 2 + 1) * DM], ones[:, :], fb2_s[:, :], start=False, stop=True),
                        S["f2mm"], [memsets])
                    yield 0.43
                yield 0
                t2 = bank.give(i, emit("dve", lambda e, r=r, ps=ps: e.tensor_tensor(
                    h1[:, r:r + 2, :], h1[:, r:r + 2, :], ps[:, :].rearrange("p (j d) -> p j d", j=2), ALU.add),
                    S["hres"], [t, ta, last["h1_T"]]))
            last["yT_read"] = t
            yield 0.2
            yield from normalize("post", h1, 1e-12, [t2])
            yield from affine(ln2_s, last["post"])
            ta = last["aff"]
            yield from until(lambda: c in moe_done)
            for r in (0, J // 2):
                yield from idle("pool")
                ta = emit("pool", lambda e, r=r: e.tensor_tensor(
                    h1[:, r:r + J // 2, :], h1[:, r:r + J // 2, :], xres[:, r:r + J // 2, :], ALU.add), S["aff"],
                    [ta, moe_done[c]])
            last["h1_out"] = emit("sync", lambda e: e.dma_start(out_c[c], h1[:, :, :]), s_out, [ta])
            if c + 1 < NC:
                xres_here[c + 1] = emit("sync", lambda e: e.dma_start(xres[:, :, :], x_c[c + 1]), s_xres, [ta])

        def load_expert(c, ex):
            i, buf, free = m1w.take()
            m1_here[ex] = i, buf, emit("sync", lambda e, buf=buf: e.dma_start(buf[:, :, :], m1[ex]), s_m1[i], [free])

        def load_expert2(c, ex):
            i, buf, free = m2w.take()
            m2_here[ex] = i, buf, emit("sync", lambda e, buf=buf: e.dma_start(buf[:, :], m2[ex]), s_m2[i], [free])

        def moe(c):
            b, r = c % 3, S["rt"]
            yield from until(lambda: c in glog_ready)
            gate_here = yield from route(c)
            t = emit("dve", lambda e: e.tensor_copy(gsp[:, :, 0:E], gate[:, :, :]), r,
                     [gate_here, last.get("gsp_read"), memsets])
            t = emit("dve", lambda e: e.tensor_tensor(grem[:, :, :], gate[:, :, :], gsp[:, :, 0:E], ALU.subtract), r, [t])
            t = emit("dve", lambda e: e.tensor_copy(gsp[:, :, DS:DS + E], grem[:, :, :]), r, [t])
            t = emit("dve", lambda e: e.tensor_tensor(gsp[:, :, 2 * DS:2 * DS + E], grem[:, :, :], gsp[:, :, DS:DS + E],
                                                      ALU.subtract), r, [t])
            yield 0
            i, ps, free = yield from some(bank)
            psb = ps[:, :].bitcast(BF16)
            for j in range(J):
                t2 = emit("pe", lambda e, j=j, psb=psb: e.transpose(
                    psb[0:SW, j * P:(j + 1) * P], gsp[:, j, :], identb[:, :]), S["gtr"], [t, free])
            last["gsp_read"] = t2
            yield 0.2
            yield 0
            bank.give(i, emit("act", lambda e, psb=psb: e.activation(
                gT[:, :], psb[0:SW, 0:T], ACT.Copy), S["gev"], [t2, last.get("gT_read")]))
            i, ps, free = yield from some(bank)
            for j in range(J):
                t2 = emit("pe", lambda e, j=j, ps=ps: e.transpose(
                    ps[0:E, j * P:(j + 1) * P], gate[:, j, :], ident[:, :]), S["gtr"], [gate_here, free])
            last["gate_read"] = t2
            yield 0.4
            yield 0
            gi, gTf, gfree = yield from some(gbuf)
            gT_here = bank.give(i, emit("act", lambda e, ps=ps: e.activation(
                gTf[0:E, :], ps[0:E, :], ACT.Copy), S["gev"], [t2, gfree]))
            yield 0
            for j in range(J):
                t = emit("pe", lambda e, j=j: e.matmul(
                    acc[:, j, :], gTf[0:E, j * P:(j + 1) * P], mb2_s[:, :], start=(j % 2 == 0), stop=False,
                    skip_group_check=True), S["m2mm"], [gT_here, last.get("acc_read"), w_rest])
            gbuf.give(gi, t)
            yield 1.7
            for e0 in range(0, E, 4):
                four = range(e0, e0 + 4)
                rows = {}
                for ex in four:
                    i, ps, free = yield from some(bank)
                    wi, wb, tw = m1_here.pop(ex)
                    for k in range(K):
                        t = emit("pe", lambda e, k=k, ps=ps, wb=wb: e.matmul(
                            ps[:, :], wb[:, k, :], xnT[b][:, k, :], start=(k == 0), stop=(k == K - 1)),
                            S["m1mm"], [xnT_ready[c], free, tw])
                        yield 0.86
                    m1w.give(wi, t)
                    last[("xnT", b)] = t
                    if ex + 2 < E or c + 1 < NC:
                        load_expert(c, (ex + 2) % E)
                    yield 0
                    hi, hb, hfree = hid.take()
                    te = bank.give(i, emit("act", lambda e, ps=ps, ex=ex, hb=hb: e.activation(
                        hb[:, :], ps[:, :], ACT.Identity, bias=mb1_s[:, ex:ex + 1]), S["m1ev"], [t, hfree]))
                    rows[ex] = hi, hb
                yield 0
                for ex in four:
                    te = emit("act", lambda e, hb=rows[ex][1]: e.activation(hb[:, :], hb[:, :], ACT.Gelu),
                              S["gelu"], [te])
                yield 0
                for ex in four:
                    hi, hb = rows[ex]
                    i, ps, free = yield from some(bank)
                    t = emit("pe", lambda e, ps=ps, ex=ex: e.matmul(ps[:, :], sel[:, ex, :], gT[:, :], start=True, stop=True),
                             S["gbc"], [gT_here, free])
                    yield 0.2
                    yield 0
                    tm = bank.give(i, emit("dve", lambda e, ps=ps, hb=hb: e.tensor_tensor(
                        hb[:, :], hb[:, :], ps[:, :], ALU.mult), S["mg"], [te, t]))
                    yield 0
                    wi, wb, tw = m2_here.pop(ex)
                    for j in range(J):
                        t = emit("pe", lambda e, j=j, hb=hb, wb=wb, ex=ex: e.matmul(
                            acc[:, j, :], hb[:, j * P:(j + 1) * P], wb[:, :], start=False,
                            stop=(ex == E - 1), skip_group_check=True), S["m2mm"], [tm, tw])
                        yield 0.43
                    hid.give(hi, t)
                    m2w.give(wi, t)
                    if ex + 5 < E or c + 1 < NC:
                        load_expert2(c, (ex + 5) % E)
            last["gT_read"] = t
            yield from until(lambda: c in xres_here)
            tx = xres_here[c]
            yield from there(tx)
            for r in range(0, J, 2):
                t2 = emit("dve", lambda e, r=r: e.tensor_tensor(
                    xres[:, r:r + 2, :], xres[:, r:r + 2, :], acc[:, r:r + 2, :], ALU.add), S["fin"], [t, tx])
                yield 0
            moe_done[c] = last["acc_read"] = t2

        def gated_T(c, j, ty):
            p = c % 2
            i, ps, free = yield from some(bank)
            for g in range(G):
                t = emit("pe", lambda e, g=g, ps=ps: e.transpose(
                    ps[:, g * P:(g + 1) * P], y[p][:, j, g * P:(g + 1) * P], ident[:, :]), S["ytr"], [ty, free])
            last[("y_read", p)] = t
            yield 0
            last["yT_w"] = bank.give(i, emit("act", lambda e, ps=ps: e.activation(
                yT[:, :, j * P:(j + 1) * P], ps[:, :].rearrange("p (g t) -> p g t", g=G), ACT.Copy), S["yev"],
                [t, last.get("yT_read")]))
            yield 0.45

        sq_ready, glog_ready = {}, {}
        xn_ready, xnT_ready, gT_ready, bT_ready, dt_ready, u_ready, y_init, moe_done = {}, {}, {}, {}, {}, {}, {}, {}
        m1_here, m2_here, routed, gated, summed = {}, {}, set(), set(), set()
        xres_here = {0: emit("sync", lambda e: e.dma_start(xres[:, :, :], x_c[0]), s_xres)}

        bbc_here, bu_here, dA_here, scan_done, hT_done, sum_done = {}, {}, {}, {}, {}, {}
        x_here[2] = load_x(2)

        def spread_b(q):
            c, n = divmod(q, DS)
            i, ps, free = bank.take()
            t = emit("pe", lambda e: e.matmul(ps[:, :], sel[:, n, :], bT[c % 2][:, :], start=True, stop=True),
                     S["bbcmm"], [bT_ready[c], free])
            last[("bT_read", c % 2)] = t
            bi, bb, bfree = bbc.take()

            def evacuate():
                te = bank.give(i, emit("act", lambda e: e.activation(bb[:, :], ps[:, :], ACT.Copy), S["bbc"], [t, bfree]))
                bbc_here[q] = bi, bb, te
            return evacuate

        def make_bu(w):
            q, half = divmod(w, G // 2)
            c = q // DS
            bi, bb, te = bbc_here[q]
            ri, rb, rfree = bu.take()
            t = emit("pool", lambda e: e.tensor_tensor(
                rb[:, :, :], xs[c % 2][:, 2 * half:2 * half + 2, :], bb[:, :].unsqueeze(1).to_broadcast([P, 2, T]),
                ALU.mult), S["bu"], [te, u_ready[c], rfree])
            if half == G // 2 - 1:
                bbc.give(bi, t)
            last[("u_read", c % 2)] = t
            bu_here[w] = ri, rb, t

        def make_dA(s):
            c, r = divmod(s, STEPS)
            n, g = divmod(r, G)
            ri, rb, rfree = dA.take()
            t = emit("act", lambda e: e.activation(rb[:, :], dt[c % 2][:, g, :], ACT.Exp, scale=nega[:, g, n:n + 1]),
                     S["dA"], [dt_ready[c], rfree, cst_neg])
            last[("dt_read", c % 2)] = t
            dA_here[s] = ri, rb, t

        def scan(s):
            c, r = divmod(s, STEPS)
            n, g = divmod(r, G)
            ai, ab, ta = dA_here.pop(s)
            wi, wb, tw = bu_here[s // 2]
            hi, hb, hfree = h.take()
            first = c % CPS == 0
            t = emit("dve", lambda e: e.tensor_tensor_scan(
                hb, ab[:, :], wb[:, s % 2, :], 0.0 if first else carry[:, n, g:g + 1], ALU.mult, ALU.add),
                S["scan"], [ta, tw, hfree, carry_wait.get(hi), None if first else carry_of[n, g]])
            dA.give(ai, t)
            if s % 2:
                bu.give(wi, t)
            if (c + 1) % CPS and s % 2:
                assert hi % 2
                carry_of[n, g - 1] = carry_of[n, g] = carry_wait[hi - 1] = carry_wait[hi] = emit("pool", lambda e: e.tensor_copy(
                    carry[:, n, g - 1:g + 1], hrows[:, hi - 1:hi + 1, T - 1]), S["carry"], [t])
            scan_done[s] = hi, hb, t

        def turn(q, j):
            bi, hb, free = hT.take()
            for g in range(G):
                hi, hs, t = scan_done[q * G + g]
                t2 = emit("pe", lambda e, g=g, hs=hs: e.transpose(hb[:, g * P:(g + 1) * P], hs[:, j * P:(j + 1) * P],
                                                                  ident[:, :]), S["hT"], [t, free])
                if j == J - 1:
                    h.give(hi, t2)
            hT_done[q, j] = bi, hb, t2

        def add_up(q, j):
            c, n = divmod(q, DS)
            bi, hb, t = hT_done.pop((q, j))
            t = emit("dve", lambda e: e.scalar_tensor_tensor(
                out=y[c % 2][:, j, :], in0=hb[:, :], scalar=xdbl[c % 2][:, j, DTR + DS + n:DTR + DS + n + 1],
                in1=y[c % 2][:, j, :], op0=ALU.mult, op1=ALU.add), S["sum"],
                [t, y_init[c], sum_done.get((q - 1, j))])
            hT.give(bi, t)
            sum_done[(q, j)] = t
            last[("C_read", c % 2)] = t
            last[("y_done", c)] = t

        carry_wait, carry_of = {}, {}

        class Side:

            def __init__(self, gen, total):
                self.gen, self.total, self.done, self.at = gen, total, 0.0, 0.0

            def step(self):
                w = next(self.gen, None)
                if w is None:
                    self.gen = None
                elif w == 0:
                    self.at = max(newest[0] + HOP, clock["dve"] + .1)
                elif w < 0:
                    self.at = clock["dve"] - w
                else:
                    self.done += w
                return w or 0

        def fill(sides, due, backlog):
            while True:
                ready = [x for x in sides if x.gen is not None and x.at <= clock["dve"]]
                if not ready:
                    break
                x = min(ready, key=lambda x: x.done / x.total - due[x])
                if clock["pe"] > clock["dve"] + (backlog if x.done / x.total >= due[x] else BM):
                    break
                x.step()

        def finish(x, sides):
            hurry.append(x)
            while x.gen is not None:
                if x.step() < 0:
                    for other in sides:
                        if other is not x and other.gen is not None:
                            other.step()
            hurry.clear()

        TAIL = 8
        PRE, ATTN, MOE = 39, 32.4, 31.5
        BL, BM = 1.5, 6.0
        LAG = 4.0
        HOP = .1
        finish(Side(pre(0), 1), [])
        for ex in range(len(m1w.bufs)):
            load_expert(0, ex)
        for ex in range(len(m2w.bufs)):
            load_expert2(0, ex)
        LB, LU, LA = 1, 2, 3
        for q in range(LB + 1):
            spread_b(q)()
        for w in range(LU):
            make_bu(w)
        for s in range(LA):
            make_dA(s)
        total = NC * STEPS
        behind = Side((w for c in range(NC) for w in attn(c)), ATTN)
        experts = Side((w for c in range(NC) for w in moe(c)), MOE)
        for c in range(NC):
            ahead = Side(pre(c + 1) if c + 1 < NC else None, PRE)
            for r in range(STEPS):
                s = c * STEPS + r
                n, g = divmod(r, G)
                q = s // G
                if s + LA < total:
                    make_dA(s + LA)
                if s % 2 == 0 and s // 2 + LU < total // 2:
                    make_bu(s // 2 + LU)
                if g == 0 and q + 2 < NC * DS:
                    evac = spread_b(q + 2)
                elif g == 1 and q + 2 < NC * DS:
                    evac()
                scan(s)
                if r == G:
                    summed.add(c - 1)
                sides = [ahead, behind, experts]
                due = {ahead: r / (STEPS - TAIL), behind: c - 1 + r / STEPS, experts: c + r / STEPS}
                fill(sides, due, BL)
                if q > 0 and g == 0:
                    turn(q - 1, 0)
                    turn(q - 1, 1)
                    if q > 1:
                        add_up(q - 2, 3)
                elif q > 0 and g == 1:
                    turn(q - 1, 2)
                    add_up(q - 1, 0)
                elif q > 0 and g == 2:
                    add_up(q - 1, 1)
                    turn(q - 1, 3)
                elif q > 0:
                    add_up(q - 1, 2)
                if r == STEPS - TAIL - 1:
                    finish(ahead, sides)
                fill(sides, due, BL)
        q = NC * DS - 1
        add_up(q - 1, 3)
        for j in range(J):
            turn(q, j)
            add_up(q, j)
        summed.add(NC - 1)
        finish(behind, [experts])
        queue["sync"].append(lambda e: e.wait_ge(s_out.sem, s_out.count))

        block = ctx.enter_context(nc.Block())

        @block.sync
        def _(eng):
            for step in queue["sync"]:
                step(eng)

        @block.tensor
        def _(eng):
            for step in queue["pe"]:
                step(eng)

        @block.vector
        def _(eng):
            for step in queue["dve"]:
                step(eng)

        @block.scalar
        def _(eng):
            for step in queue["act"]:
                step(eng)

        @block.gpsimd
        def _(eng):
            for step in queue["pool"]:
                step(eng)


def kernel(**inputs):
    import ml_dtypes
    import concourse.bacc as bacc
    from concourse.bass_utils import run_bass_kernel_spmd

    a = {k: np.asarray(v) for k, v in inputs.items()}
    A, M = "L0_attn_", "L0_ffn_"

    def rows(w, p=P):
        return np.ascontiguousarray(w.reshape(-1, p, *w.shape[1:]).swapaxes(0, 1))

    def every(*vs):
        return np.ascontiguousarray(np.broadcast_to(np.stack(vs), (P, len(vs), vs[0].shape[0])))

    ds = a[A + "A_log"].shape[1]
    sel = np.zeros((3 * ds, ds, P), np.float32)
    for r in range(3 * ds):
        sel[r, r % ds, :] = 1.0
    bf = ml_dtypes.bfloat16
    arrays = {
        "x": a[A + "x"],
        "win": rows(a[A + "in_proj_w"].T),
        "wconv": rows(a[A + "conv_w"]),
        "bconv": rows(a[A + "conv_b"]),
        "wx": rows(a[A + "x_proj_w"].T),
        "wdt": np.concatenate([a[A + "dt_proj_w"].T, a[A + "dt_proj_b"][None]], 0),
        "alog": rows(a[A + "A_log"]),
        "dvec": rows(a[A + "D"]),
        "wout": rows(a[A + "out_proj_w"].T),
        "ln1": every(a[A + "ln1_w"], a[A + "ln1_b"]),
        "f1": rows(a[A + "ffn_w1"].T),
        "fb1": rows(a[A + "ffn_b1"]),
        "f2": rows(a[A + "ffn_w2"].T),
        "fb2": a[A + "ffn_b2"][None],
        "ln2": every(a[A + "ln2_w"], a[A + "ln2_b"]),
        "m1": a[M + "w1"].reshape(a[M + "w1"].shape[0], -1, P, P).transpose(0, 2, 1, 3),
        "mb1": np.ascontiguousarray(a[M + "b1"].T),
        "m2": a[M + "w2"],
        "mb2": a[M + "b2"],
        "cent": a[M + "centroids"],
        "wroute": rows(a[M + "w_route"].T),
        "ident": np.eye(P, dtype=np.float32),
        "identb": np.eye(P, dtype=np.float32).astype(bf),
        "sel": sel.astype(bf),
    }
    nc = bacc.Bacc("TRN2", target_bir_lowering=False, num_devices=1)
    arrays = {k: np.ascontiguousarray(v) for k, v in arrays.items()}
    args = [nc.dram_tensor(f"in_{k}", v.shape, mybir.dt.from_np(v.dtype), kind="ExternalInput").ap()
            for k, v in arrays.items()]
    out = nc.dram_tensor("out_y", a[A + "x"].shape, F32, kind="ExternalOutput").ap()
    build_block(nc, *args, out)
    r = run_bass_kernel_spmd(nc, [{f"in_{k}": v for k, v in arrays.items()}], core_ids=[0])
    return r.results[0]["out_y"]
```
